# Optimizing a Trainium2 kernel written in Bass

```python
import numpy as np
import jax
import jax.numpy as jnp

def _softmax(x, axis=-1):
    return jax.nn.softmax(x, axis=axis)

def _gelu(x):
    return jax.nn.gelu(x, approximate=True)

def _silu(x):
    return jax.nn.silu(x)

def _sigmoid(x):
    return jax.nn.sigmoid(x)

def _layernorm(x, axis=-1, eps=1e-05):
    m = jnp.mean(x, axis=axis, keepdims=True)
    v = jnp.var(x, axis=axis, keepdims=True)
    return (x - m) / jnp.sqrt(v + eps)

def _scatter_add(tgt, idx, src, axis=0):
    return tgt.at[idx].add(src)

def _segment_sum(src, seg, n):
    return jax.ops.segment_sum(src, seg, n)
kernel_name = 'mk_decoder_preln_d1_seqx_r2_578019'

def setup_inputs(seed: int=0):
    np.random.seed(seed)
    _w = jnp.asarray

    def _rec_inputs():
        import jax
        import jax.numpy as jnp
        _rk = jax.random.key(seed)
        x = 7.22e-05 + 1 * jax.random.normal(jax.random.fold_in(_rk, 1), (8, 512, 512), jnp.float32)
        _lenS = 512 - jax.random.randint(jax.random.fold_in(_rk, 7), (8,), 0, max(1, 512 // 4) + 1, jnp.int32)
        _lenS2 = 512 - jax.random.randint(jax.random.fold_in(_rk, 8), (8,), 0, max(1, 512 // 4) + 1, jnp.int32)
        _ctx_1024P = jax.random.normal(jax.random.fold_in(_rk, 11), (8, 16, 512), jnp.float32)
        _ctx_1024c = jax.random.dirichlet(jax.random.fold_in(_rk, 511), 0.3 * jnp.ones((16,), jnp.float32), (8, 512))
        _ctx_1024t = jnp.einsum('bsk,bkd->bsd', _ctx_1024c, _ctx_1024P)
        _ctx_1024t = _ctx_1024t * jax.lax.rsqrt(jnp.mean(jnp.square(_ctx_1024t)) + 1e-12) * 0.953939
        ctx_1024 = 4.13588e-05 + 0.999923 * (_ctx_1024t + 0.3 * jax.random.normal(jax.random.fold_in(_rk, 611), (8, 512, 512), jnp.float32))
        _validS = jnp.arange(512)[None, :] < _lenS[:, None]
        _validS2 = jnp.arange(512)[None, :] < _lenS2[:, None]
        _causal = jnp.tril(jnp.ones((512, 512), dtype=bool))
        mask_BxS2_bk0 = jnp.logical_not(jnp.broadcast_to(_validS2[:, :], (8, 512)))
        return (x, ctx_1024, mask_BxS2_bk0)
    x, ctx_1024, mask_BxS2_bk0 = _rec_inputs()

    def _L0_attn_setup():
        import math
        import jax, jax.numpy as jnp
        import numpy as np
        B, S, D, H = (4, 1024, 512, 16)
        HD = D // H
        key = jax.random.key(seed)
        k1, k2, k3 = jax.random.split(key, 3)
        x = jax.random.normal(k1, (B, S, D), dtype=jnp.float32)
        w_qkv = jax.random.normal(k2, (D, 3 * D), dtype=jnp.float32) * (1.0 / math.sqrt(D))
        b_qkv = jnp.zeros((3 * D,), dtype=jnp.float32)
        w_dense = jax.random.normal(k3, (D, D), dtype=jnp.float32) * (1.0 / math.sqrt(D))
        b_dense = jnp.zeros((D,), dtype=jnp.float32)
        return {'x': x, 'w_qkv': w_qkv, 'b_qkv': b_qkv, 'w_dense': w_dense, 'b_dense': b_dense}
    _L0_attn_all = _L0_attn_setup()
    _L0_attn_in = {k: v for k, v in _L0_attn_all.items() if k in ('w_qkv', 'b_qkv', 'w_dense', 'b_dense')}
    del _L0_attn_all

    def _L0_xattn_setup():
        import jax, jax.numpy as jnp
        import numpy as np
        B, S, D, H = (4, 1024, 512, 16)
        DH = D // H
        key = jax.random.key(seed)
        ks = jax.random.split(key, 12)
        scale = 1.0 / np.sqrt(D)
        inp = {'query': jax.random.normal(ks[0], (B, S, D), jnp.float32), 'key': jax.random.normal(ks[1], (B, S, D), jnp.float32), 'value': jax.random.normal(ks[2], (B, S, D), jnp.float32), 'key_padding_mask': jax.random.randint(ks[3], (B, S), 0, 2).astype(bool), 'Wq': jax.random.normal(ks[4], (D, H * DH), jnp.float32) * scale, 'bq': jnp.zeros((H * DH,), jnp.float32), 'Wk': jax.random.normal(ks[5], (D, H * DH), jnp.float32) * scale, 'bk': jnp.zeros((H * DH,), jnp.float32), 'Wv': jax.random.normal(ks[6], (D, H * DH), jnp.float32) * scale, 'bv': jnp.zeros((H * DH,), jnp.float32), 'Wo': jax.random.normal(ks[7], (H * DH, D), jnp.float32) * scale, 'bo': jnp.zeros((D,), jnp.float32)}
        return inp
    _L0_xattn_all = _L0_xattn_setup()
    _L0_xattn_in = {k: v for k, v in _L0_xattn_all.items() if k in ('Wq', 'bq', 'Wk', 'bk', 'Wv', 'bv', 'Wo', 'bo')}
    del _L0_xattn_all

    def _L0_ffn_setup():
        import jax, jax.numpy as jnp
        import numpy as np
        D = 512
        E = 8
        key = jax.random.key(seed)
        ks = jax.random.split(key, 7)
        s = 1.0 / np.sqrt(D)
        x = jax.random.normal(ks[0], (4, 1024, D), dtype=jnp.float32)
        Wg = jax.random.uniform(ks[1], (D, E), minval=-s, maxval=s, dtype=jnp.float32)
        bg = jax.random.uniform(ks[2], (E,), minval=-s, maxval=s, dtype=jnp.float32)
        W1 = jax.random.uniform(ks[3], (E, D, D), minval=-s, maxval=s, dtype=jnp.float32)
        b1 = jax.random.uniform(ks[4], (E, D), minval=-s, maxval=s, dtype=jnp.float32)
        W2 = jax.random.uniform(ks[5], (E, D, D), minval=-s, maxval=s, dtype=jnp.float32)
        b2 = jax.random.uniform(ks[6], (E, D), minval=-s, maxval=s, dtype=jnp.float32)
        return {'x': x, 'Wg': Wg, 'bg': bg, 'W1': W1, 'b1': b1, 'W2': W2, 'b2': b2}
    _L0_ffn_all = _L0_ffn_setup()
    _L0_ffn_in = {k: v for k, v in _L0_ffn_all.items() if k in ('Wg', 'bg', 'W1', 'b1', 'W2', 'b2')}
    del _L0_ffn_all
    return {'x': x, 'ctx_1024': ctx_1024, 'mask_BxS2_bk0': mask_BxS2_bk0, 'L0_attn_w_qkv': _L0_attn_in['w_qkv'], 'L0_attn_b_qkv': _L0_attn_in['b_qkv'], 'L0_attn_w_dense': _L0_attn_in['w_dense'], 'L0_attn_b_dense': _L0_attn_in['b_dense'], 'L0_xattn_Wq': _L0_xattn_in['Wq'], 'L0_xattn_bq': _L0_xattn_in['bq'], 'L0_xattn_Wk': _L0_xattn_in['Wk'], 'L0_xattn_bk': _L0_xattn_in['bk'], 'L0_xattn_Wv': _L0_xattn_in['Wv'], 'L0_xattn_bv': _L0_xattn_in['bv'], 'L0_xattn_Wo': _L0_xattn_in['Wo'], 'L0_xattn_bo': _L0_xattn_in['bo'], 'L0_ffn_Wg': _L0_ffn_in['Wg'], 'L0_ffn_bg': _L0_ffn_in['bg'], 'L0_ffn_W1': _L0_ffn_in['W1'], 'L0_ffn_b1': _L0_ffn_in['b1'], 'L0_ffn_W2': _L0_ffn_in['W2'], 'L0_ffn_b2': _L0_ffn_in['b2']}

def reference(x, ctx_1024, mask_BxS2_bk0, L0_attn_w_qkv, L0_attn_b_qkv, L0_attn_w_dense, L0_attn_b_dense, L0_xattn_Wq, L0_xattn_bq, L0_xattn_Wk, L0_xattn_bk, L0_xattn_Wv, L0_xattn_bv, L0_xattn_Wo, L0_xattn_bo, L0_ffn_Wg, L0_ffn_bg, L0_ffn_W1, L0_ffn_b1, L0_ffn_W2, L0_ffn_b2):
    import jax
    import jax.numpy as jnp

    def _L0_attn_ref(x, w_qkv, b_qkv, w_dense, b_dense):
        import math
        import jax, jax.numpy as jnp
        import numpy as np
        B, S, D, H = (4, 1024, 512, 16)
        HD = D // H
        b, s, d = x.shape
        qkv = x @ w_qkv + b_qkv
        qkv = qkv.reshape(b, s, H, 3 * HD).transpose(0, 2, 1, 3)
        q, k, v = jnp.split(qkv, 3, axis=-1)
        scores = jnp.einsum('bhqd,bhkd->bhqk', q, k) / math.sqrt(HD)
        causal = jnp.tril(jnp.ones((s, s), dtype=bool))[None, None, :, :]
        scores = jnp.where(causal, scores, jnp.asarray(-10000.0, dtype=scores.dtype))
        probs = jax.nn.softmax(scores, axis=-1)
        ctx = jnp.einsum('bhqk,bhkd->bhqd', probs, v)
        ctx = ctx.transpose(0, 2, 1, 3).reshape(b, s, d)
        out = ctx @ w_dense + b_dense
        return out

    def _L0_xattn_ref(query, key, value, key_padding_mask, Wq, bq, Wk, bk, Wv, bv, Wo, bo):
        import jax, jax.numpy as jnp
        import numpy as np
        B, S, D, H = (4, 1024, 512, 16)
        DH = D // H
        b, nq, _ = query.shape
        nk = key.shape[-2]
        q = (query @ Wq + bq).reshape(b, nq, H, DH).transpose(0, 2, 1, 3)
        k = (key @ Wk + bk).reshape(b, nk, H, DH).transpose(0, 2, 1, 3)
        v = (value @ Wv + bv).reshape(b, nk, H, DH).transpose(0, 2, 1, 3)
        scores = jnp.einsum('bhqd,bhkd->bhqk', q, k) / np.sqrt(DH)
        mask = key_padding_mask[:, None, None, :]
        scores = jnp.where(mask, -jnp.inf, scores)
        w = jax.nn.softmax(scores, axis=-1)
        attn = jnp.einsum('bhqk,bhkd->bhqd', w, v)
        attn = attn.transpose(0, 2, 1, 3).reshape(b, nq, H * DH)
        return attn @ Wo + bo

    def _L0_ffn_ref(x, Wg, bg, W1, b1, W2, b2):
        import jax, jax.numpy as jnp
        import numpy as np
        D = 512
        E = 8
        N, T, d = x.shape
        x_flat = x.reshape(N * T, d)
        logits = x_flat @ Wg + bg
        probs = jax.nn.softmax(logits, axis=-1)
        assignments = jnp.argmax(probs, axis=-1)
        h = jnp.einsum('nd,edh->neh', x_flat, W1) + b1[None]
        h = jax.nn.gelu(h, approximate=False)
        eo = jnp.einsum('neh,ehd->ned', h, W2) + b2[None]
        selected = jnp.take_along_axis(eo, assignments[:, None, None], axis=1)[:, 0, :]
        w = jnp.take_along_axis(probs, assignments[:, None], axis=1)
        out = (w * selected).reshape(N, T, d)
        return out
    x = x + _L0_attn_ref(_layernorm(x, axis=-1), L0_attn_w_qkv, L0_attn_b_qkv, L0_attn_w_dense, L0_attn_b_dense)
    x = x + _L0_xattn_ref(_layernorm(x, axis=-1), ctx_1024, ctx_1024, mask_BxS2_bk0, L0_xattn_Wq, L0_xattn_bq, L0_xattn_Wk, L0_xattn_bk, L0_xattn_Wv, L0_xattn_bv, L0_xattn_Wo, L0_xattn_bo)
    x = x + _L0_ffn_ref(_layernorm(x, axis=-1), L0_ffn_Wg, L0_ffn_bg, L0_ffn_W1, L0_ffn_b1, L0_ffn_W2, L0_ffn_b2)
    return x

_drawn_inputs = setup_inputs


def setup_inputs(seed=0):
    import zlib

    import numpy as np

    out = dict(_drawn_inputs(seed))
    spreads = {'L0_attn_b_qkv': (0.0, 0.1),
     'L0_attn_b_dense': (0.0, 0.1),
     'L0_xattn_bq': (0.0, 0.408),
     'L0_xattn_bk': (0.0, 2.0),
     'L0_xattn_bv': (0.0, 0.1),
     'L0_xattn_bo': (0.0, 0.1)}
    factors = {'L0_ffn_bg': 7.356, 'L0_ffn_b1': 27.667, 'L0_ffn_b2': 8.0}
    for name, (base, spread) in spreads.items():
        noise = np.random.default_rng([zlib.crc32(name.encode()), seed]).standard_normal(out[name].shape)
        drawn = base * np.exp(spread * noise) if base else spread * noise
        out[name] = jnp.asarray(drawn.astype(out[name].dtype))
    for name, factor in factors.items():
        out[name] = (out[name] * factor).astype(out[name].dtype)
    return out
```

```python
import concourse.bass as bass
from concourse import mybir
from contextlib import ExitStack

ALU = mybir.AluOpType
ACT = mybir.ActivationFunctionType
AX_X = mybir.AxisListType.X
F32 = mybir.dt.float32
F32R = mybir.dt.float32r
BF16 = mybir.dt.bfloat16
I32 = mybir.dt.int32
U8 = mybir.dt.uint8

P = 128
B, S, D = 8, 512, 512
H, HD = 16, 32
KT = D // P
NB = S // P
G, J = 4, 4
N_EXPERT = 8
EPS = 1e-5
LOWEST = -(2.0 ** 100)
SCALE = float(HD) ** -0.5
ROW_MASK, ROW_MAX = 96, 97
SPLIT = ((0, 0), (0, 1), (1, 0))


def attention_layer(nc, name, causal, x_in, x_out, ctx_in, mask_in, scratch_mask,
                    load_weights, load_biases, b_out):
    cross = ctx_in is not None
    order = [("Tc", t) for t in range(NB)] if cross else []
    order += [("q", 0), ("k", 0), ("q", 1), ("k", 1), ("v", 0), ("q", 2), ("k", 2), ("q", 3), ("k", 3),
              ("v", 1), ("mT", 0), ("v", 2), ("v", 3)]
    order += [("mT", 1), ("bc", 0), ("mT", 2), ("bc", 1), ("mT", 3), ("bc", 2)]
    order += [("Tx", t) for t in range(NB)] + [("bc", 3)] + [("wo", t) for t in range(NB)]
    N_ITEM = len(order)
    PRO = NB
    at = {key: PRO + i for i, key in enumerate(order)}
    his = [key for key in order if key[0] in ("Tc", "Tx", "q", "k")]
    N_HI = len(his)
    hi_at = {key: NB + i for i, key in enumerate(his)}
    N_STACK = 3 * J + (1 if cross else 0)
    S_AHEAD = 4
    S_PER_KB = (5, 4, 3, 0)

    with ExitStack() as ctx:
        def sb(nm, shape, dt=F32):
            return ctx.enter_context(nc.sbuf_tensor(f"{name}_{nm}", shape, dt))

        def ps(nm, shape):
            return ctx.enter_context(nc.psum_tensor(f"{name}_{nm}", shape, F32))

        def sem(nm):
            return ctx.enter_context(nc.semaphore(f"{name}_{nm}"))

        W = [sb("w_high", [P, KT, 4, D], F32R), sb("w_low", [P, KT, 4, D], F32R)]
        stack = sb("stack", [P, G, 2, J, S], F32R)
        xT = [sb("xT_high", [P, KT, S], F32R), sb("xT_low", [P, KT, S], F32R)]
        oT = [sb("oT_high", [P, KT, S], F32R), sb("oT_low", [P, KT, S], F32R)]
        kvT = oT if cross else xT
        V = sb("V", [P, NB, D])
        probs = sb("probs", [P, 2, J, S])
        stage = sb("stage", [P, 4, S], F32R)
        xb = sb("xb", [P, NB, D])
        o_sb = sb("o_sb", [P, S])
        bo = sb("bo", [P, D])
        ident = sb("ident", [P, P])
        onehot = sb("onehot", [P, HD + NB - 1])
        m_neg = sb("m_neg", [J * NB, P], F32R)
        m_col = sb("m_col", [P, 2, J * NB])
        rec = sb("rec", [P, P])
        bias = sb("bias", [P, 3, G])
        stats = sb("stats", [P, NB, 6])
        mv = sb("mv", [P, NB, 2])
        ln_const = sb("ln_const", [P, 3, NB])
        rstd = sb("rstd", [P, NB])
        nmr = sb("nmr", [P, NB])
        if not cross:
            tri = sb("tri", [P, 2 * S - P], BF16)

        pj = ps("pj", [P, 2, S])
        sS = ps("sS", [P, 2, S])
        sT = ps("sT", [P, 2, S])
        o_ps = ps("o_ps", [P, S])
        den = ps("den", [P, S])

        raw_loaded = [sem("raw_loaded_0"), sem("raw_loaded_1")]
        raw_high, raw_done = sem("raw_high"), sem("raw_done")
        const_loaded, const_step = sem("const_loaded"), sem("const_step")
        mask_loaded, mask_ready, mask_stored = sem("mask_loaded"), sem("mask_ready"), sem("mask_stored")
        x_loaded, ctx_loaded, resid_loaded = sem("x_loaded"), sem("ctx_loaded"), sem("resid_loaded")
        stacked = [sem("stacked_even"), sem("stacked_odd")]
        max_stacked, stored = sem("max_stacked"), sem("stored")
        ln_stats, ln_step, ln_ready, xn_ready = sem("ln_stats"), sem("ln_step"), sem("ln_ready"), sem("xn_ready")
        dve_step = sem("dve_step")
        pool_waited, dve_waited, sp_waited = sem("pool_waited"), sem("dve_waited"), sem("sp_waited")
        pj_full, pj_free, high_done = sem("pj_full"), sem("pj_free"), sem("high_done")
        s_full, s_free = sem("s_full"), sem("s_free")
        st_full, exp_done, masked, pv_done = sem("st_full"), sem("exp_done"), sem("masked"), sem("pv_done")
        o_copied, rec_ready, oT_high, oT_ready = sem("o_copied"), sem("rec_ready"), sem("oT_high"), sem("oT_ready")
        resid_ready = sem("resid_ready")

        def filled(b, key):
            return N_ITEM * b + (at[key] + 1)

        def bank_free(b, key):
            return N_ITEM * b + (at[key] + 1)

        def all_stacked(b, g):
            return 16 * N_STACK * 2 * b + 16 * N_STACK * (g // 2 + 1)

        def taken(b, key):
            return N_ITEM * b + (at[key] + 3)

        stage_f32, stack_f32 = stage[:].bitcast(F32), stack[:].bitcast(F32)
        split_qk = [stage[:], xb[:].bitcast(F32R)]
        split_f32 = [stage_f32, xb[:]]
        probs_flat = probs[:].rearrange("p a j s -> p (a j s)")
        x_rows = x_in.rearrange("b (t p) d -> b p t d", p=P)
        out_rows = x_out.rearrange("b (t p) d -> b p t d", p=P)
        ctx_rows = ctx_in.rearrange("b (t p) d -> b p t d", p=P) if cross else None
        weights = load_weights()
        mask_f32 = probs[0:B, 1, 0, :]
        mask_u8 = probs[0:B, 1, 1, 0:S // 4].bitcast(U8)
        N_CONST = 4 if cross else 13
        N_STEP = 8 if cross else 11
        PV0 = G * NB
        block = ctx.enter_context(nc.Block())

        def weight_views(i):
            src, to, of = weights[i]
            raw = probs_flat[:, (i % 2) * J * S:(i % 2 + 1) * J * S]
            return src, raw, [to(W[h]) for h in range(2)], of(raw)

        def raw_dst(raw, src):
            n = 1
            for s in src.shape[1:]:
                n *= s
            r = raw[:, 0:n]
            return r if len(src.shape) == 2 else r.rearrange("p (t d) -> p t d", t=src.shape[1])

        @block.sync
        def _(sp):
            load_biases(nc, sp, bias, const_loaded)
            sp.dma_start(bo[:], b_out.partition_broadcast(P)).then_inc(const_loaded, 16)
            if cross:
                sp.dma_start(mask_u8.bitcast(I32), mask_in).then_inc(mask_loaded, 16)
                sp.wait_ge(mask_ready, 1)
                sp.dma_start(scratch_mask, mask_f32).then_inc(mask_stored, 16)
                sp.wait_ge(mask_stored, 16)
            sp.dma_start(xb[:], x_rows[0]).then_inc(x_loaded, 16)
            for i in range(len(weights)):
                if i >= 2:
                    sp.wait_ge(raw_done, i - 1)
                src, raw, _, _ = weight_views(i)
                sp.dma_start(raw_dst(raw, src), src).then_inc(raw_loaded[i % 2], 16)
            if cross:
                sp.wait_ge(raw_done, len(weights))
                sp.dma_start(probs[:, 0], ctx_rows[0]).then_inc(ctx_loaded, 16)

            def stack_group(b, g):
                sp.wait_ge(pj_free, taken(b, ("k", g)))
                sp.sem_inc(sp_waited, 1)
                sp.wait_ge(pv_done, PV0 * b + NB * (g + 1))
                of, done = split_f32[g % 2], stacked[g % 2]
                for j in range(J):
                    rows = slice(HD * j, HD * (j + 1))
                    sp.dma_start(stack_f32[0:HD, g, :, j], of[rows, 1:3]).then_inc(done, 16)
                    sp.dma_start(stack_f32[HD:2 * HD, g, :, j], of[rows, 0:3:2]).then_inc(done, 16)
                    sp.dma_start(stack_f32[2 * HD:3 * HD, g, :, j], of[rows, 1:4:2]).then_inc(done, 16)
                if cross:
                    sp.dma_start(stack_f32[ROW_MASK:ROW_MASK + 1, g, 1],
                                 scratch_mask[bass.ds(b, 1)].unsqueeze(1).broadcast_to([1, J, S])).then_inc(done, 16)

            def stack_max(b, g):
                sp.wait_ge(pj_free, taken(b, ("mT", g)))
                sp.dma_start(stack_f32[ROW_MAX:ROW_MAX + 1, g, 0].rearrange("o j s -> o (j s)"), m_neg[:].bitcast(F32)).then_inc(max_stacked, 16)

            with sp.Fori(0, B) as b:
                nxt = sp.snap((b + 1) % B)
                for g in range(G):
                    stack_group(b, g)
                stack_max(b, 0)
                sp.wait_ge(stacked[0], all_stacked(b, 2))
                sp.sem_inc(sp_waited, 1)
                sp.dma_start(stage_f32, x_rows[b]).then_inc(resid_loaded, 16)
                sp.wait_ge(stacked[1], all_stacked(b, 3))
                sp.sem_inc(sp_waited, 1)
                sp.dma_start(xb[:], x_rows[nxt]).then_inc(x_loaded, 16)
                for g in range(1, G):
                    stack_max(b, g)
                if cross:
                    sp.wait_ge(pv_done, PV0 * b + (PV0 + PV0 - 1))
                    sp.sem_inc(sp_waited, 1)
                    sp.dma_start(probs[:, 0], ctx_rows[nxt]).then_inc(ctx_loaded, 16)
                for t in range(NB):
                    sp.wait_ge(pj_free, taken(b, ("wo", t)))
                    sp.sem_inc(sp_waited, 1)
                    sp.dma_start(out_rows[b][:, t], stage_f32[:, t]).then_inc(stored, 16)
            sp.wait_ge(stored, 16 + 16 * NB * B)
            if cross:
                sp.wait_ge(ctx_loaded, 16 * (B + 1))

        @block.gpsimd
        def _(pool):
            pool.sem_inc(pj_free, 2)
            pool.sem_inc(s_free, 2)
            pool.sem_inc(exp_done, 2)
            pool.sem_inc(pv_done, PV0)
            pool.sem_inc(o_copied, 1)
            pool.sem_inc(rec_ready, 1)
            pool.sem_inc(oT_ready, 1)
            pool.sem_inc(stored, 16)
            pool.sem_inc(max_stacked, 16)
            pool.memset(ident[:], 0.0).then_inc(const_step, 1)
            pool.memset(onehot[:], 0.0).then_inc(const_step, 1)
            for n, value in enumerate((EPS, -0.5, -1.0)):
                pool.memset(ln_const[:, n], value).then_inc(const_step, 1)
            pool.wait_ge(const_step, 5)
            pool.memset(stack_f32[ROW_MASK:ROW_MAX + 1], 1.0).then_inc(const_step, 1)
            pool.wait_ge(const_step, 6)
            pool.affine_select(out=ident[:], in_=ident[:], compare_op=ALU.not_equal, fill=1.0, base=0,
                               pattern=[[-1, P]], channel_multiplier=1).then_inc(const_step, 1)
            pool.memset(onehot[:, NB - 1::NB], 1.0).then_inc(const_step, 1)
            if not cross:
                pool.wait_ge(const_step, 8)
                pool.memset(stack_f32[ROW_MASK:ROW_MASK + 1, :, 1], 0.0).then_inc(const_step, 1)
                pool.wait_ge(const_step, 9)
                pool.memset(tri[:], 0.0).then_inc(const_step, 1)
                pool.wait_ge(const_step, 10)
                pool.affine_select(out=tri[:], in_=tri[:], compare_op=ALU.is_ge, fill=LOWEST, base=S - P,
                                   pattern=[[-1, 2 * S - P]], channel_multiplier=1).then_inc(const_step, 1)
            else:
                pool.wait_ge(mask_loaded, 16)
                pool.tensor_scalar(mask_f32, mask_u8, LOWEST, None, ALU.mult).then_inc(mask_ready, 1)

            def layernorm_scale(b):
                pool.wait_ge(ln_stats, b + 1)
                pool.tensor_tensor(rstd[:], mv[:, :, 1], ln_const[:, 0], ALU.add).then_inc(ln_step, 1)
                pool.wait_ge(ln_step, 3 * b + 1)
                pool.tensor_tensor(rstd[:], rstd[:], ln_const[:, 1], ALU.pow).then_inc(ln_step, 1)
                pool.wait_ge(ln_step, 3 * b + 2)
                pool.tensor_tensor(nmr[:], mv[:, :, 0], rstd[:], ALU.mult).then_inc(ln_step, 1)
                pool.wait_ge(ln_step, 3 * b + 3)
                pool.tensor_tensor(nmr[:], nmr[:], ln_const[:, 2], ALU.mult).then_inc(ln_ready, 1)

            layernorm_scale(0)
            with pool.Fori(0, B) as b:
                for g in range(G):
                    for kb in range(NB):
                        if not cross:
                            pool.wait_ge(exp_done, G * NB * J * b + (2 + (g * NB + kb + 1) * J))
                            pool.sem_inc(pool_waited, 1)
                            diag = probs[:, kb % 2, :, kb * P:(kb + 1) * P]
                            pool.affine_select(out=diag, in_=diag, compare_op=ALU.is_ge, fill=0.0, base=0,
                                               pattern=[[0, J], [1, P]], channel_multiplier=-1).then_inc(masked, 1)
                        if g == 2 and kb == 1:
                            layernorm_scale(b + 1)
                pool.wait_ge(resid_loaded, 16 * b + 16)
                for t in range(NB):
                    pool.tensor_tensor(stage_f32[:, t], stage_f32[:, t], bo[:], ALU.add).then_inc(resid_ready, 1)

        @block.scalar
        def _(act):
            for i in range(len(weights)):
                act.wait_ge(raw_loaded[i % 2], 16 * (i // 2 + 1))
                _, _, (high, _), raw = weight_views(i)
                act.copy(high, raw).then_inc(raw_high, 1)

            def normalize(b):
                act.wait_ge(ln_ready, b + 1)
                for t in range(NB):
                    act.activation(xb[:, t], xb[:, t], ACT.Identity, scale=rstd[:, t:t + 1],
                                   bias=nmr[:, t:t + 1]).then_inc(xn_ready, 1)

            def high_of_transposed(to, idx, bank, t):
                act.wait_ge(pj_full, idx + 1)
                act.copy(to[0][:, :, t * P:(t + 1) * P],
                         pj[:, bank].rearrange("p (k s) -> p k s", k=KT)).then_inc(high_done, 1)

            def high_of_qk(b, which, g):
                if which == 0 and g == 0:
                    act.wait_ge(stored, 16 * NB * b + 16)
                elif which == 0 and g >= 2:
                    act.wait_ge(stacked[g % 2], all_stacked(b, g - 2))
                i = at["qk"[which], g]
                act.wait_ge(pj_full, filled(b, ("qk"[which], g)))
                act.activation(split_qk[g % 2][:, 1 + which], pj[:, i % 2], ACT.Identity,
                               bias=bias[:, which, g:g + 1]).then_inc(high_done, 1)

            def attend(b, g):
                for kb in range(NB):
                    q0 = kb * P if not cross else 0
                    act.wait_ge(pv_done, PV0 * b + (PV0 + g * NB + kb - 1))
                    for j in range(J):
                        n = (g * NB + kb) * J + j
                        act.wait_ge(st_full, G * NB * J * b + (n + 1))
                        act.activation(probs[:, kb % 2, j, q0:S], sT[:, n % 2, q0:S], ACT.Exp,
                                       scale=SCALE).then_inc(exp_done, 1)
                    if kb == 2 and g >= 1:
                        high_of_output(b, g - 1)
                act.wait_ge(oT_ready, G * b + (g + 1))
                act.wait_ge(pv_done, PV0 * b + (PV0 + (g + 1) * NB))
                act.copy(o_sb[:], o_ps[:]).then_inc(o_copied, 1)

            def high_of_output(b, g):
                act.wait_ge(pj_free, taken(b, ("bc", g)))
                act.activation(oT[0][:, g], o_sb[:], ACT.Identity, bias=bias[:, 2, g:g + 1]).then_inc(oT_high, 1)

            act.wait_ge(const_loaded, 16 * N_CONST)
            normalize(0)
            for t in range(NB):
                high_of_transposed(xT, t, t % 2, t)
            with act.Fori(0, B) as b:
                if cross:
                    for t in range(NB):
                        high_of_transposed(oT, N_ITEM * b + at["Tc", t], at["Tc", t] % 2, t)
                for g in range(G):
                    for which in range(2):
                        high_of_qk(b, which, g)
                for g in range(G):
                    attend(b, g)
                    if g == 2:
                        normalize(b + 1)
                for t in range(NB):
                    high_of_transposed(xT, N_ITEM * b + at["Tx", t], at["Tx", t] % 2, t)
                high_of_output(b, G - 1)

        @block.vector
        def _(dve):
            for i in range(len(weights)):
                dve.wait_ge(raw_high, i + 1)
                _, _, (high, low), raw = weight_views(i)
                dve.tensor_tensor(low, raw, high.bitcast(F32), ALU.subtract).then_inc(raw_done, 1)

            def row_stats(b):
                dve.wait_ge(x_loaded, 16 * b + 16)
                for t in range(NB):
                    dve.bn_stats(stats[:, t], xb[:, t]).then_inc(dve_step, 1)
                for t in range(NB):
                    dve.wait_ge(dve_step, NB * b + (t + 1))
                    dve.sem_inc(dve_waited, 1)
                    last = dve.bn_aggr(mv[:, t], stats[:, t])
                last.then_inc(ln_stats, 1)

            def low_of_transposed(to, bank, nh, t):
                dve.wait_ge(high_done, nh + 1)
                cols = slice(t * P, (t + 1) * P)
                dve.tensor_tensor(to[1][:, :, cols], pj[:, bank].rearrange("p (k s) -> p k s", k=KT),
                                  to[0][:, :, cols].bitcast(F32), ALU.subtract).then_inc(pj_free, 1)

            def low_of_qk(b, which, g):
                i = at["qk"[which], g]
                dve.wait_ge(high_done, N_HI * b + (hi_at["qk"[which], g] + 1))
                op = dve.scalar_tensor_tensor(out=split_qk[g % 2][:, 3 * which], in0=pj[:, i % 2], scalar=bias[:, which, g:g + 1],
                                              in1=split_f32[g % 2][:, 1 + which], op0=ALU.add, op1=ALU.subtract)
                op.then_inc(pj_free, 1)

            def copy_v(b, t):
                i = at["v", t]
                dve.wait_ge(pj_full, N_ITEM * b + (i + 1))
                dve.tensor_copy(V[:, t], pj[:, i % 2]).then_inc(pj_free, 1)

            def maxima(b, g, first, count):
                for n in range(first, first + count):
                    j, qb = n // NB, n % NB
                    m = g * J * NB + n
                    dve.wait_ge(s_full, G * J * NB * b + (m + 1))
                    to = m_col[:, g % 2, n:n + 1]
                    if cross:
                        op = dve.tensor_reduce(to, sS[:, m % 2], AX_X, ALU.max)
                    else:
                        width = (qb + 1) * P
                        dve.sem_inc(dve_waited, 1)
                        op = dve.tensor_tensor_reduce(sS[:, m % 2, 0:width], sS[:, m % 2, 0:width],
                                                      tri[:, S - P - qb * P:S - P - qb * P + width],
                                                      1.0, LOWEST, ALU.add, ALU.max, to)
                    op.then_inc(s_free, 1)

            def negate_max(b, g):
                i = at["mT", g]
                dve.wait_ge(pj_full, filled(b, ("mT", g)))
                dve.wait_ge(max_stacked, 16 * G * b + 16 * (g + 1))
                dve.tensor_scalar(m_neg[:], pj[0:J * NB, i % 2, 0:P], -1.0, None, ALU.mult).then_inc(pj_free, 1)

            def reciprocals(b, g):
                dve.wait_ge(pv_done, PV0 * b + (PV0 + (g + 1) * NB))
                dve.reciprocal(rec[:], den[:, 0:P]).then_inc(rec_ready, 1)

            def divide(b, g):
                i = at["bc", g]
                dve.wait_ge(o_copied, G * b + (g + 2))
                dve.wait_ge(pj_full, filled(b, ("bc", g)))
                dve.tensor_tensor(o_sb[:], pj[:, i % 2], o_sb[:], ALU.mult).then_inc(pj_free, 1)

            def low_of_output(b, g):
                dve.wait_ge(oT_high, G * b + (g + 1))
                dve.scalar_tensor_tensor(out=oT[1][:, g], in0=o_sb[:], scalar=bias[:, 2, g:g + 1],
                                         in1=oT[0][:, g].bitcast(F32), op0=ALU.add, op1=ALU.subtract).then_inc(oT_ready, 1)

            def add_rows(b, t):
                i = at["wo", t]
                dve.wait_ge(resid_ready, NB * b + (t + 1))
                dve.wait_ge(pj_full, N_ITEM * b + (i + 1))
                dve.tensor_tensor(stage_f32[:, t], pj[:, i % 2], stage_f32[:, t], ALU.add).then_inc(pj_free, 1)

            dve.wait_ge(const_loaded, 16 * N_CONST)
            dve.wait_ge(const_step, N_STEP)
            row_stats(0)
            for t in range(NB):
                low_of_transposed(xT, t % 2, t, t)
            with dve.Fori(0, B) as b:
                if cross:
                    for t in range(NB):
                        low_of_transposed(oT, at["Tc", t] % 2, N_HI * b + hi_at["Tc", t], t)
                for g in range(2):
                    for which in range(2):
                        low_of_qk(b, which, g)
                copy_v(b, 0)
                for n, (which, g) in enumerate([(0, 2), (1, 2), (0, 3), (1, 3)]):
                    maxima(b, 0, n * NB, NB)
                    low_of_qk(b, which, g)
                copy_v(b, 1)
                negate_max(b, 0)
                copy_v(b, 2)
                copy_v(b, 3)
                for g in range(G):
                    if g + 1 < G:
                        maxima(b, g + 1, 0, S_AHEAD)
                    if g == 2:
                        row_stats(b + 1)
                    for kb in range(NB):
                        if g + 1 < G:
                            maxima(b, g + 1, S_AHEAD + sum(S_PER_KB[:kb]), S_PER_KB[kb])
                        if kb == 1 and g >= 1:
                            divide(b, g - 1)
                        if kb == 3 and g + 1 < G:
                            negate_max(b, g + 1)
                        if kb == 3 and g >= 1:
                            low_of_output(b, g - 1)
                    reciprocals(b, g)
                for t in range(NB):
                    low_of_transposed(xT, at["Tx", t] % 2, N_HI * b + hi_at["Tx", t], t)
                divide(b, G - 1)
                low_of_output(b, G - 1)
                for t in range(NB):
                    add_rows(b, t)

        @block.tensor
        def _(pe):
            def transposes(rows, idx, bank):
                pe.wait_ge(pj_free, idx + 1)
                for k in range(KT):
                    op = pe.transpose(pj[:, bank, k * P:(k + 1) * P], rows[:, k * P:(k + 1) * P], ident[:])
                op.then_inc(pj_full, 1)

            def split_product(out, a_of, b_of, start, stop, between=None):
                ops = None
                for k in range(KT):
                    for n, (x, y) in enumerate(SPLIT):
                        ops = pe.matmul(out, a_of(x, k), b_of(y, k), start=start and k == 0 and n == 0,
                                        stop=stop and k == KT - 1 and n == len(SPLIT) - 1)
                    if between is not None:
                        between(k)
                return ops

            def project_qk(b, which, g, between=None):
                i = at["qk"[which], g]
                pe.wait_ge(pj_free, N_ITEM * b + (i + 1))
                src = xT if which == 0 else kvT
                split_product(pj[:, i % 2], lambda x, k: W[x][:, k, which, g * P:(g + 1) * P],
                              lambda y, k: src[y][:, k], True, True, between).then_inc(pj_full, 1)

            def project_v(b, t):
                i = at["v", t]
                pe.wait_ge(pj_free, N_ITEM * b + (i + 1))
                split_product(pj[:, i % 2], lambda x, k: kvT[x][:, k, t * P:(t + 1) * P],
                              lambda y, k: W[y][:, k, 2], True, True).then_inc(pj_full, 1)

            def scores(b, g, n):
                j, qb = n // NB, n % NB
                m = g * J * NB + n
                width = S if cross else max((qb + 1) * P, 2 * P)
                pe.wait_ge(s_free, G * J * NB * b + (m + 1))
                pe.matmul(sS[:, m % 2, 0:width], stack[0:ROW_MAX, g, 0, j, qb * P:(qb + 1) * P],
                          stack[0:ROW_MAX, g, 1, j, 0:width], start=True, stop=True).then_inc(s_full, 1)

            def max_rows(b, g):
                i = at["mT", g]
                pe.wait_ge(pj_free, N_ITEM * b + (i + 1))
                pe.wait_ge(s_free, G * J * NB * b + (2 + (g + 1) * J * NB))
                pe.transpose(pj[0:J * NB, i % 2, 0:P], m_col[:, g % 2], ident[:]).then_inc(pj_full, 1)

            def scores_T(b, g, kb, j):
                q0 = min(kb * P, S - 2 * P) if not cross else 0
                n = (g * NB + kb) * J + j
                pe.wait_ge(exp_done, G * NB * J * b + (n + 1))
                pe.matmul(sT[:, n % 2, q0:S], stack[0:ROW_MAX + 1, g, 1, j, kb * P:(kb + 1) * P],
                          stack[0:ROW_MAX + 1, g, 0, j, q0:S], start=True, stop=True).then_inc(st_full, 1)

            def weighted_values(b, g, kb):
                q0 = kb * P if not cross else 0
                if kb == 0:
                    pe.wait_ge(o_copied, G * b + (g + 1))
                    pe.wait_ge(rec_ready, G * b + (g + 1))
                pe.wait_ge(exp_done, G * NB * J * b + (2 + (g * NB + kb + 1) * J))
                if not cross:
                    pe.wait_ge(masked, G * NB * b + (g * NB + kb + 1))
                for j in range(J):
                    cols = slice((g * J + j) * HD, (g * J + j + 1) * HD)
                    pe.matmul(o_ps[HD * j:HD * (j + 1), q0:S], V[:, kb, cols], probs[:, kb % 2, j, q0:S],
                              start=kb == 0, stop=kb == NB - 1)
                for qb in range(q0 // P, NB):
                    pick = onehot[:, NB - 1 - qb:NB - 1 - qb + HD]
                    for j in range(J):
                        op = pe.matmul(den[HD * j:HD * (j + 1), 0:P], pick, probs[:, kb % 2, j, qb * P:(qb + 1) * P],
                                       start=kb == 0 and qb == 0, stop=kb == NB - 1 and qb == NB - 1)
                op.then_inc(pv_done, 1)

            def spread_reciprocals(b, g):
                i = at["bc", g]
                pe.wait_ge(pj_free, N_ITEM * b + (i + 1))
                pe.wait_ge(rec_ready, G * b + (g + 2))
                for qb in range(NB):
                    for j in range(J):
                        pick = ident[:, HD * j + qb:HD * j + qb + 1].broadcast_to([P, HD])
                        op = pe.matmul(pj[HD * j:HD * (j + 1), i % 2, qb * P:(qb + 1) * P], pick, rec[:],
                                       start=True, stop=True)
                op.then_inc(pj_full, 1)

            def attend(b, g):
                if g + 1 < G:
                    pe.wait_ge(stacked[(g + 1) % 2], all_stacked(b, g + 1))
                    for n in range(S_AHEAD):
                        scores(b, g + 1, n)
                pe.wait_ge(max_stacked, 16 * G * b + (16 + 16 * (g + 1)))
                for j in range(J):
                    scores_T(b, g, 0, j)
                done = S_AHEAD
                for kb in range(NB):
                    ahead = list(range(done, done + S_PER_KB[kb])) if g + 1 < G else []
                    done += S_PER_KB[kb]
                    if kb == 1 and g >= 1:
                        spread_reciprocals(b, g - 1)
                    if kb == 3 and g + 1 < G:
                        max_rows(b, g + 1)
                    for j in range(J):
                        if j < len(ahead):
                            scores(b, g + 1, ahead[j])
                        if kb + 1 < NB:
                            scores_T(b, g, kb + 1, j)
                    weighted_values(b, g, kb)
                    for n in ahead[J:]:
                        scores(b, g + 1, n)

            def out_projection(b, t, gs):
                i = at["wo", t]
                for g in gs:
                    for n, (x, y) in enumerate(SPLIT):
                        op = pe.matmul(pj[:, i % 2], oT[x][:, g, t * P:(t + 1) * P], W[y][:, g, 3],
                                       start=g == 0 and n == 0, stop=g == G - 1 and n == len(SPLIT) - 1)
                if G - 1 in gs:
                    op.then_inc(pj_full, 1)

            pe.wait_ge(const_step, N_STEP)
            pe.wait_ge(raw_done, len(weights))
            for t in range(NB):
                pe.wait_ge(xn_ready, t + 1)
                transposes(xb[:, t], t, t % 2)
            pe.wait_ge(pj_free, PRO + 2)
            with pe.Fori(0, B) as b:
                pe.wait_ge(pj_free, taken(b - 1, ("Tx", NB - 1)))
                if cross:
                    pe.wait_ge(ctx_loaded, 16 * b + 16)
                    for t in range(NB):
                        transposes(probs[:, 0, t], N_ITEM * b + at["Tc", t], at["Tc", t] % 2)
                    pe.wait_ge(pj_free, taken(b, ("Tc", NB - 1)))
                for g in range(2):
                    project_qk(b, 0, g)
                    project_qk(b, 1, g)
                project_v(b, 0)
                pe.wait_ge(stacked[0], all_stacked(b, 0))
                for n, (which, g) in enumerate([(0, 2), (1, 2), (0, 3), (1, 3)]):
                    project_qk(b, which, g, lambda k, n=n: scores(b, 0, n * NB + k))
                project_v(b, 1)
                max_rows(b, 0)
                project_v(b, 2)
                project_v(b, 3)
                pe.wait_ge(pj_free, taken(b, ("v", 3)))
                for g in range(G):
                    attend(b, g)
                pe.wait_ge(xn_ready, NB * b + 2 * NB)
                for t in range(NB):
                    transposes(xb[:, t], N_ITEM * b + at["Tx", t], at["Tx", t] % 2)
                spread_reciprocals(b, G - 1)
                pe.wait_ge(oT_ready, G * b + G)
                for t in range(2):
                    pe.wait_ge(pj_free, bank_free(b, ("wo", t)))
                    out_projection(b, t, range(G - 1))
                pe.wait_ge(oT_ready, G * b + (G + 1))
                for t in range(2):
                    out_projection(b, t, range(G - 1, G))
                for t in range(2, NB):
                    pe.wait_ge(pj_free, bank_free(b, ("wo", t)))
                    out_projection(b, t, range(G))


def expert_layer(nc, x_in, x_out, Wg, bg, W1, b1, W2, b2):
    N = B * S
    NT = N // P
    E = N_EXPERT
    TOK = 2 * P
    R = TOK // P
    RING = 3
    most = (N + E * (TOK - 1)) // TOK
    TILES = -(-most // RING) * RING
    COLS = (TILES + RING) * R
    REC = 4
    SLOTS = P * COLS
    CH = 2
    KC = KT // CH
    with ExitStack() as ctx:
        def sb(nm, shape, dt=F32):
            return ctx.enter_context(nc.sbuf_tensor(f"moe_{nm}", shape, dt))

        def ps(nm, shape):
            return ctx.enter_context(nc.psum_tensor(f"moe_{nm}", shape, F32))

        def sem(nm):
            return ctx.enter_context(nc.semaphore(f"moe_{nm}"))

        def sems(nm):
            return [sem(f"{nm}_{i}") for i in range(RING)]

        records = nc.dram_tensor("records", (SLOTS, REC), F32).ap()
        W_all = [sb("w1", [P, E, KT, D]), sb("w2", [P, E, KT, D])]
        w1 = [sb("w1_high", [P, KT, D], F32R), sb("w1_low", [P, KT, D], F32R)]
        w2 = [sb("w2_high", [P, KT, D], F32R), sb("w2_low", [P, KT, D], F32R)]
        rows = sb("rows", [P, RING, R, D])
        xn = sb("xn", [P, R, D])
        xT = [sb("xT_high", [P, KT, TOK], F32R), sb("xT_low", [P, KT, TOK], F32R)]
        h = sb("h", [P, KT, TOK])
        hT = [sb("hT_high", [P, KT, TOK], F32R), sb("hT_low", [P, KT, TOK], F32R)]
        b2_rows = sb("b2_rows", [P, RING, D])
        wb2 = sb("wb2", [P, R, D])
        b1_cols = sb("b1_cols", [P, E, KT])
        rec_all = sb("rec_all", [P, COLS, REC])
        cur = sb("cur", [P, RING, R, REC])
        tile_expert = sb("tile_expert", [P, TILES + 1], I32)
        ident = sb("ident", [P, P])
        ln_const = sb("ln_const", [P, 3, NB])
        gx = [W_all[1][:, E - 2 + half] for half in range(2)]
        gxT = [wb2[:, n] for n in range(2)]
        wg = xn[:, 0].rearrange("p (k c) -> p k c", k=KT)[:, :, 0:E]
        desk = rows[:].rearrange("p a r d -> p (a r d)")
        earlier, ones = desk[:, 0:P], desk[:, P:2 * P]
        stats = desk[:, 256:256 + 2 * NB * 6].rearrange("p (a t s) -> p a t s", a=2, t=NB)
        mv = desk[:, 320:320 + 2 * NB * 2].rearrange("p (a t s) -> p a t s", a=2, t=NB)
        rstd = desk[:, 352:352 + 2 * NB].rearrange("p (a t) -> p a t", a=2)
        nmr = desk[:, 376:376 + 2 * NB].rearrange("p (a t) -> p a t", a=2)
        rec_tok = b2_rows[:, 0, 0:NT * REC].rearrange("p (t r) -> p t r", t=NT)
        slot_i = b2_rows[:, 0, NT * REC:NT * REC + NT].bitcast(I32)
        pad = b2_rows[:, 1, 0:COLS * REC].rearrange("p (c r) -> p c r", c=COLS)
        bg_rows = b2_rows[:, 1, 256:256 + E]
        prefer = b2_rows[:, 1, 288:288 + E]
        tile_no = b2_rows[:, 1, 320:320 + TILES + 1]
        b1_rows = b2_rows[0:E * KT, 2, 0:P]

        def table(flat, n):
            return flat[:, n * NT * E:(n + 1) * NT * E].rearrange("p (t e) -> p t e", e=E)
        logits, less, expd, hot = [table(h[:].rearrange("p k s -> p (k s)"), n) for n in range(4)]
        cand, *scan = [table(desk, n) for n in range(2, 5)]
        past = desk[:, 1280:1280 + (TILES + 1) * E].rearrange("p (t e) -> p t e", e=E)
        top, first, total, place, col_f = [desk[:, 1536 + n * NT:1536 + (n + 1) * NT] for n in range(5)]
        place_i, col_i, row_i = [desk[:, 1792 + n * NT:1792 + (n + 1) * NT].bitcast(I32) for n in range(3)]
        count, tiles_of, ends, ends2, start = [desk[:, 2048 + n * E:2048 + (n + 1) * E] for n in range(5)]
        count_i, tiles_i = [desk[:, 2112 + n * E:2112 + (n + 1) * E].bitcast(I32) for n in range(2)]
        te_f = desk[:, 2176:2176 + TILES + 1]

        pT = ps("pT", [P, 2, D])
        hidden = ps("hidden", [P, KT, 2 * TOK])
        ph = hidden[:, :, 0:TOK]
        py = ps("py", [P, R, D])
        lg = [hidden[:, half, 0:NB * E].rearrange("p (t e) -> p t e", e=E) for half in range(2)]
        rank, totals = [hidden[:, 2 + n, 0:NT * E].rearrange("p (t e) -> p t e", e=E) for n in range(2)]

        const_step, const_loaded, wg_loaded = sem("const_step"), sem("const_loaded"), sem("wg_loaded")
        pad_stored, weights_loaded = sem("pad_stored"), sem("weights_loaded")
        gx_loaded = [sem("gx_loaded_0"), sem("gx_loaded_1")]
        g_bn, g_stats, g_step, g_ln = sem("g_bn"), sem("g_stats"), sem("g_step"), sem("g_ln")
        g_norm, g_full, g_copied = sem("g_norm"), sem("g_full"), sem("g_copied")
        g_logits, g_taken, b1_full, b1_ready = sem("g_logits"), sem("g_taken"), sem("b1_full"), sem("b1_ready")
        route, less_ready, exp_ready, hot_ready, ranked = (sem("route"), sem("less_ready"), sem("exp_ready"),
                                                           sem("hot_ready"), sem("ranked"))
        slots_ready, experts_ready = sem("slots_ready"), sem("experts_ready")
        rec_stored, rec_loaded = sem("rec_stored"), sem("rec_loaded")
        rows_set, cur_ready = sem("rows_set"), sem("cur_ready")
        gathered, scattered, b2_loaded = sems("gathered"), sems("scattered"), sems("b2_loaded")
        w1_high, w1_low, w2_high, w2_low = sem("w1_high"), sem("w1_low"), sem("w2_high"), sem("w2_low")
        normed, t_full, xT_high, xT_low = sem("normed"), sem("t_full"), sem("xT_high"), sem("xT_low")
        h_full, gelu_done, h_high, h_low = sem("h_full"), sem("gelu_done"), sem("h_high"), sem("h_low")
        y_full, y_taken, resid_ready = sem("y_full"), sem("y_taken"), sem("resid_ready")
        wb2_ready = sem("wb2_ready")
        pool_waited, dve_waited, sp_waited, act_waited = (sem("pool_waited"), sem("dve_waited"),
                                                          sem("sp_waited"), sem("act_waited"))

        x_batches = x_in.rearrange("b (t p) d -> b p t d", p=P)
        x_tokens = x_in.rearrange("b s d -> (b s) d")
        out_tokens = x_out.rearrange("b s d -> (b s) d")
        N_CONST = 8
        block = ctx.enter_context(nc.Block())

        @block.sync
        def _(sp):
            for half in range(2):
                sp.dma_start(gx[half], x_batches[half]).then_inc(gx_loaded[half], 16)
            with nc.allow_non_contiguous_dma("the gate's weights, rows of 32 bytes, once"):
                sp.dma_start(wg, Wg.rearrange("(k p) e -> p k e", p=P)).then_inc(wg_loaded, 16)
            sp.dma_start(bg_rows, bg.partition_broadcast(P)).then_inc(const_loaded, 16)
            sp.dma_start(b1_rows, b1.rearrange("e (k p) -> (e k) p", p=P)).then_inc(const_loaded, 16)
            sp.wait_ge(const_step, N_CONST)
            sp.dma_start(records.rearrange("(p c) r -> p c r", p=P), pad).then_inc(pad_stored, 16)
            with sp.Fori(0, B // 2 - 1) as pair:
                for half in range(2):
                    sp.wait_ge(g_full, 2 * NB * pair + NB * (half + 1))
                    sp.sem_inc(sp_waited, 1)
                    sp.dma_start(gx[half], x_batches[2 * pair + (2 + half)]).then_inc(gx_loaded[half], 16)
            sp.wait_ge(rec_stored, 16 * NT)
            sp.dma_start(rec_all[:], records.rearrange("(p c) r -> p c r", p=P)).then_inc(rec_loaded, 16)
            sp.wait_ge(experts_ready, 1)
            with sp.Fori(0, TILES // RING) as lap:
                for i in range(RING):
                    sp.wait_ge(resid_ready, R * RING * lap + R * (i + 1))
                    sp.sem_inc(sp_waited, 1)
                    e = sp.value_load(tile_expert[0:1, bass.ds(RING * lap + i, 1)], min_val=0, max_val=E - 1)
                    sp.dma_start(b2_rows[:, i], b2[bass.ds(e, 1)].rearrange("o d -> (o d)").partition_broadcast(P)).then_inc(b2_loaded[i], 16)
            for i in range(RING):
                sp.wait_ge(scattered[i], 16 * R * (TILES // RING))
                sp.wait_ge(gathered[i], 16 * R * (TILES // RING + 1))

        @block.gpsimd
        def _(pool):
            pool.sem_inc(g_copied, 2)
            pool.sem_inc(g_taken, 2)
            pool.sem_inc(resid_ready, R * RING)
            pool.sem_inc(y_full, R)
            pool.sem_inc(y_taken, R)
            pool.memset(ident[:], 0.0).then_inc(const_step, 1)
            pool.memset(earlier, 1.0).then_inc(const_step, 1)
            pool.memset(ones, 1.0).then_inc(const_step, 1)
            for n, value in enumerate((EPS, -0.5, -1.0)):
                op = pool.memset(ln_const[:, n], value)
            op.then_inc(const_step, 1)
            pool.memset(pad, 0.0).then_inc(const_step, 1)
            pool.wait_ge(const_step, 5)
            pool.affine_select(out=ident[:], in_=ident[:], compare_op=ALU.not_equal, fill=1.0, base=0,
                               pattern=[[-1, P]], channel_multiplier=1).then_inc(const_step, 1)
            pool.affine_select(out=earlier, in_=earlier, compare_op=ALU.is_ge, fill=0.0, base=-1,
                               pattern=[[1, P]], channel_multiplier=-1).then_inc(const_step, 1)
            pool.iota(pad[:, :, 0].bitcast(I32), pattern=[[1, COLS]], base=N, channel_multiplier=COLS).then_inc(const_step, 1)
            pool.iota(rec_tok[:, :, 0].bitcast(I32), pattern=[[P, NT]], base=0, channel_multiplier=1).then_inc(route, 1)
            for e in range(E):
                pool.memset(prefer[:, e:e + 1], float(E - e)).then_inc(route, 1)
            for t in range(TILES + 1):
                pool.memset(tile_no[:, t:t + 1], float(t)).then_inc(route, 1)

            def layernorm_scale(b, half):
                pool.wait_ge(g_stats, b + 1)
                pool.tensor_tensor(rstd[:, half], mv[:, half, :, 1], ln_const[:, 0], ALU.add).then_inc(g_step, 1)
                pool.wait_ge(g_step, 3 * b + 1)
                pool.tensor_tensor(rstd[:, half], rstd[:, half], ln_const[:, 1], ALU.pow).then_inc(g_step, 1)
                pool.wait_ge(g_step, 3 * b + 2)
                pool.tensor_tensor(nmr[:, half], mv[:, half, :, 0], rstd[:, half], ALU.mult).then_inc(g_step, 1)
                pool.wait_ge(g_step, 3 * b + 3)
                pool.tensor_tensor(nmr[:, half], nmr[:, half], ln_const[:, 2], ALU.mult).then_inc(g_ln, 1)

            with pool.Fori(0, B // 2) as pair:
                for half in range(2):
                    layernorm_scale(2 * pair + half, half)

            pool.wait_ge(pad_stored, 16)
            pool.wait_ge(slots_ready, 1)
            for t in range(NT):
                pool.indirect_dma_start(records, bass.IndirectOffsetOnAxis(ap=slot_i[:, t:t + 1], axis=0),
                                        rec_tok[:, t], None, bounds_check=SLOTS - 1,
                                        oob_is_err=False).then_inc(rec_stored, 16)
            pool.wait_ge(rows_set, 1)
            pool.wait_ge(rec_loaded, 16)

            def gather(t, i):
                pool.tensor_copy(cur[:, i], rec_all[:, bass.ds(t * R, R)]).then_inc(cur_ready, 1)
                pool.wait_ge(cur_ready, t + 1)
                pool.sem_inc(pool_waited, 1)
                for r in range(R):
                    pool.indirect_dma_start(rows[:, i, r], None, x_tokens,
                                            bass.IndirectOffsetOnAxis(ap=cur[:, i, r, 0:1].bitcast(I32), axis=0),
                                            bounds_check=N - 1, oob_is_err=False).then_inc(gathered[i], 16)

            for t in range(RING):
                gather(t, t)
            with pool.Fori(0, TILES // RING) as lap:
                for i in range(RING):
                    t = RING * lap + i
                    pool.wait_ge(b2_loaded[i], 16 * lap + 16)
                    pool.wait_ge(normed, R * t + R)
                    pool.sem_inc(pool_waited, 1)
                    for r in range(R):
                        pool.tensor_scalar(wb2[:, r], b2_rows[:, i], cur[:, i, r, 1:2], None, ALU.mult).then_inc(wb2_ready, 1)
                    for r in range(R):
                        pool.wait_ge(wb2_ready, R * t + (r + 1))
                        pool.tensor_tensor(rows[:, i, r], rows[:, i, r], wb2[:, r], ALU.add).then_inc(resid_ready, 1)
                    for r in range(R):
                        pool.wait_ge(y_taken, R * t + (R + r + 1))
                        pool.sem_inc(pool_waited, 1)
                        pool.indirect_dma_start(out_tokens, bass.IndirectOffsetOnAxis(ap=cur[:, i, r, 0:1].bitcast(I32), axis=0),
                                                rows[:, i, r], None, bounds_check=N - 1,
                                                oob_is_err=False).then_inc(scattered[i], 16)
                    pool.wait_ge(scattered[i], 16 * R * lap + 16 * R)
                    pool.sem_inc(pool_waited, 1)
                    gather(t + RING, i)

        @block.scalar
        def _(act):
            def load_weights(m, e):
                act.dma_start(W_all[m][:, e], (W1, W2)[m][e].rearrange("(k p) d -> p k d", p=P)).then_inc(weights_loaded, 16)

            for e in range(E):
                load_weights(0, e)
                if e < E - 2:
                    load_weights(1, e)
            act.wait_ge(b1_full, 1)
            act.copy(b1_cols[:].rearrange("p e k -> p (e k)"), py[:, 0, 0:E * KT]).then_inc(b1_ready, 1)
            with act.Fori(0, B // 2) as pair:
                for half in range(2):
                    b = 2 * pair + half
                    act.wait_ge(g_ln, b + 1)
                    for t in range(NB):
                        act.activation(gx[half][:, t], gx[half][:, t], ACT.Identity, scale=rstd[:, half, t:t + 1],
                                       bias=nmr[:, half, t:t + 1]).then_inc(g_norm, 1)
                    for t in range(NB):
                        act.wait_ge(g_full, NB * b + (t + 1))
                        act.wait_ge(g_logits, NB * b + (t - 1 + 2))
                        act.copy(gxT[t % 2], pT[:, t % 2]).then_inc(g_copied, 1)
            act.wait_ge(g_full, N // P)
            load_weights(1, E - 2)
            load_weights(1, E - 1)
            act.wait_ge(less_ready, 1)
            act.activation(expd, less, ACT.Exp).then_inc(exp_ready, 1)

            def split_high(W, to, e, done):
                for c in range(CH):
                    ks = slice(c * KC, (c + 1) * KC)
                    act.copy(to[0][:, ks], W[:, bass.ds(e, 1), ks].rearrange("p o k d -> p (o k) d")).then_inc(done, 1)

            def expert(t):
                return act.value_load(tile_expert[0:1, bass.ds(t, 1)], min_val=0, max_val=E - 1)

            def normalize(t, i, laps):
                act.wait_ge(gathered[i], 16 * R * laps + 16 * R)
                for r in range(R):
                    act.activation(xn[:, r], rows[:, i, r], ACT.Identity, scale=cur[:, i, r, 2:3],
                                   bias=cur[:, i, r, 3:4]).then_inc(normed, 1)

            def high_of_x(t):
                for r in range(R):
                    act.wait_ge(t_full, R * t + (r + 1))
                    act.copy(xT[0][:, :, r * P:(r + 1) * P], pT[:, r].rearrange("p (k s) -> p k s", k=KT)).then_inc(xT_high, 1)

            act.wait_ge(experts_ready, 1)
            act.wait_ge(weights_loaded, 16 * 2 * E)
            split_high(W_all[0], w1, expert(0), w1_high)
            normalize(0, 0, 0)
            high_of_x(0)
            with act.Fori(0, TILES // RING) as lap:
                for i in range(RING):
                    t = RING * lap + i
                    act.wait_ge(y_full, R * t + R)
                    act.sem_inc(act_waited, 1)
                    e = expert(t)
                    split_high(W_all[1], w2, e, w2_high)
                    normalize(t + 1, (i + 1) % RING, lap + (i + 1) // RING)
                    for f in range(KT):
                        act.wait_ge(h_full, KT * t + (f + 1))
                        act.sem_inc(act_waited, 1)
                        act.activation(h[:, f], ph[:, f], ACT.Gelu,
                                       bias=b1_cols[:, bass.ds(e, 1), f]).then_inc(gelu_done, 1)
                        act.wait_ge(gelu_done, KT * t + (f + 1))
                        act.copy(hT[0][:, f], h[:, f]).then_inc(h_high, 1)
                    split_high(W_all[0], w1, expert(t + 1), w1_high)
                    high_of_x(t + 1)

        @block.vector
        def _(dve):
            dve.wait_ge(const_loaded, 32)
            dve.wait_ge(route, 1 + E + TILES + 1)
            def row_stats(b, half, loads):
                dve.wait_ge(gx_loaded[half], 16 * loads + 16)
                for t in range(NB):
                    dve.bn_stats(stats[:, half, t], gx[half][:, t]).then_inc(g_bn, 1)
                for t in range(NB):
                    dve.wait_ge(g_bn, NB * b + (t + 1))
                    dve.sem_inc(dve_waited, 1)
                    op = dve.bn_aggr(mv[:, half, t], stats[:, half, t])
                op.then_inc(g_stats, 1)

            def take_gate(b, half):
                dve.wait_ge(g_ln, b + 1)
                dve.sem_inc(dve_waited, 1)
                dve.tensor_copy(rec_tok[:, bass.ds(b * NB, NB), 2], rstd[:, half])
                dve.tensor_copy(rec_tok[:, bass.ds(b * NB, NB), 3], nmr[:, half])
                dve.wait_ge(g_logits, NB * b + (NB + 2))
                dve.sem_inc(dve_waited, 1)
                dve.tensor_tensor(logits[:, bass.ds(b * NB, NB)], lg[half],
                                  bg_rows.unsqueeze(1).broadcast_to([P, NB, E]), ALU.add).then_inc(g_taken, 1)

            row_stats(0, 0, 0)
            with dve.Fori(0, B // 2 - 1) as pair:
                for half in range(2):
                    b = 2 * pair + half
                    row_stats(b + 1, 1 - half, pair + half)
                    take_gate(b, half)
            row_stats(B - 1, 1, B // 2 - 1)
            for half in range(2):
                take_gate(B - 2 + half, half)

            def over_experts(a):
                return a.unsqueeze(2).broadcast_to([P, NT, E])

            def over_tiles(a):
                return a.unsqueeze(1).broadcast_to([P, NT, E])

            R0 = 1 + E + TILES + 1
            dve.wait_ge(g_taken, 2 + B)
            dve.tensor_reduce(top, logits, AX_X, ALU.max).then_inc(route, 1)
            dve.wait_ge(route, R0 + 1)
            dve.tensor_tensor(less, logits, over_experts(top), ALU.subtract).then_inc(less_ready, 1)
            dve.wait_ge(less_ready, 1)
            dve.tensor_scalar(cand, less, 0.0, None, ALU.is_equal).then_inc(route, 1)
            dve.wait_ge(route, R0 + 2)
            dve.tensor_tensor(cand, cand, over_tiles(prefer), ALU.mult).then_inc(route, 1)
            dve.wait_ge(route, R0 + 3)
            dve.tensor_reduce(first, cand, AX_X, ALU.max).then_inc(route, 1)
            dve.wait_ge(route, R0 + 4)
            dve.tensor_tensor(hot, over_tiles(prefer), over_experts(first), ALU.is_equal).then_inc(hot_ready, 1)
            dve.wait_ge(exp_ready, 1)
            dve.tensor_reduce(total, expd, AX_X, ALU.add).then_inc(route, 1)
            dve.wait_ge(route, R0 + 5)
            dve.reciprocal(rec_tok[:, :, 1], total).then_inc(route, 1)
            dve.wait_ge(ranked, 1)
            dve.tensor_copy(scan[0], totals).then_inc(route, 1)
            now, n, reach = 0, R0 + 7, 1
            while reach < NT:
                dve.wait_ge(route, n)
                dve.tensor_copy(scan[1 - now][:, 0:reach], scan[now][:, 0:reach]).then_inc(route, 1)
                dve.tensor_tensor(scan[1 - now][:, reach:NT], scan[now][:, reach:NT], scan[now][:, 0:NT - reach],
                                  ALU.add).then_inc(route, 1)
                now, n, reach = 1 - now, n + 2, 2 * reach
            dve.wait_ge(route, n)
            dve.tensor_scalar(count, scan[now][:, NT - 1], float(TOK - 1), None, ALU.add).then_inc(route, 1)
            dve.wait_ge(route, n + 1)
            dve.tensor_copy(count_i, count).then_inc(route, 1)
            dve.wait_ge(route, n + 2)
            dve.tensor_scalar(tiles_i, count_i, TOK.bit_length() - 1, None, ALU.arith_shift_right).then_inc(route, 1)
            dve.wait_ge(route, n + 3)
            dve.tensor_copy(tiles_of, tiles_i).then_inc(route, 1)
            dve.wait_ge(route, n + 4)
            dve.tensor_copy(ends, tiles_of).then_inc(route, 1)
            n, both, now_e, reach = n + 5, [ends, ends2], 0, 1
            while reach < E:
                dve.wait_ge(route, n)
                dve.tensor_copy(both[1 - now_e][:, 0:reach], both[now_e][:, 0:reach]).then_inc(route, 1)
                dve.tensor_tensor(both[1 - now_e][:, reach:E], both[now_e][:, reach:E], both[now_e][:, 0:E - reach],
                                  ALU.add).then_inc(route, 1)
                now_e, n, reach = 1 - now_e, n + 2, 2 * reach
            dve.wait_ge(route, n)
            end = both[now_e]
            dve.tensor_tensor(start, end, tiles_of, ALU.subtract).then_inc(route, 1)
            dve.wait_ge(route, n + 1)
            dve.tensor_scalar(start, start, float(TOK), None, ALU.mult).then_inc(route, 1)
            dve.tensor_tensor(cand, scan[now], totals, ALU.subtract).then_inc(route, 1)
            dve.wait_ge(route, n + 3)
            dve.tensor_tensor(cand, cand, rank, ALU.add).then_inc(route, 1)
            dve.wait_ge(route, n + 4)
            dve.tensor_tensor(cand, cand, over_tiles(start), ALU.add).then_inc(route, 1)
            dve.wait_ge(route, n + 5)
            dve.tensor_tensor(cand, cand, hot, ALU.mult).then_inc(route, 1)
            dve.wait_ge(route, n + 6)
            dve.tensor_reduce(place, cand, AX_X, ALU.add).then_inc(route, 1)
            dve.wait_ge(route, n + 7)
            dve.tensor_copy(place_i, place).then_inc(route, 1)
            dve.wait_ge(route, n + 8)
            dve.tensor_scalar(col_i, place_i, P.bit_length() - 1, None, ALU.arith_shift_right).then_inc(route, 1)
            dve.tensor_scalar(row_i, place_i, P - 1, None, ALU.bitwise_and).then_inc(route, 1)
            dve.wait_ge(route, n + 10)
            dve.tensor_copy(col_f, col_i).then_inc(route, 1)
            dve.tensor_copy(place, row_i).then_inc(route, 1)
            dve.wait_ge(route, n + 12)
            dve.tensor_scalar(place, place, float(COLS), None, ALU.mult).then_inc(route, 1)
            dve.wait_ge(route, n + 13)
            dve.tensor_tensor(place, place, col_f, ALU.add).then_inc(route, 1)
            dve.wait_ge(route, n + 14)
            dve.tensor_copy(slot_i, place).then_inc(slots_ready, 1)
            dve.tensor_tensor(past, tile_no.unsqueeze(2).broadcast_to([P, TILES + 1, E]),
                              end.unsqueeze(1).broadcast_to([P, TILES + 1, E]), ALU.is_ge).then_inc(route, 1)
            dve.wait_ge(route, n + 15)
            dve.tensor_reduce(te_f, past, AX_X, ALU.add).then_inc(route, 1)
            dve.wait_ge(route, n + 16)
            dve.tensor_scalar(te_f, te_f, float(E - 1), None, ALU.min).then_inc(route, 1)
            dve.wait_ge(route, n + 17)
            dve.tensor_copy(tile_expert[:], te_f).then_inc(experts_ready, 1)
            dve.wait_ge(experts_ready, 1)
            dve.memset(rows[:], 0.0).then_inc(rows_set, 1)

            def split_low(W, to, e, high, low, t):
                for c in range(CH):
                    dve.wait_ge(high, CH * t + (c + 1))
                    dve.sem_inc(dve_waited, 1)
                    ks = slice(c * KC, (c + 1) * KC)
                    dve.tensor_tensor(to[1][:, ks], W[:, bass.ds(e, 1), ks].rearrange("p o k d -> p (o k) d"),
                                      to[0][:, ks].bitcast(F32), ALU.subtract).then_inc(low, 1)

            def expert(t):
                return dve.value_load(tile_expert[0:1, bass.ds(t, 1)], min_val=0, max_val=E - 1)

            def low_of_x(t):
                for r in range(R):
                    dve.wait_ge(xT_high, R * t + (r + 1))
                    dve.tensor_tensor(xT[1][:, :, r * P:(r + 1) * P], pT[:, r].rearrange("p (k s) -> p k s", k=KT),
                                      xT[0][:, :, r * P:(r + 1) * P].bitcast(F32), ALU.subtract).then_inc(xT_low, 1)

            dve.wait_ge(experts_ready, 1)
            split_low(W_all[0], w1, expert(0), w1_high, w1_low, 0)
            low_of_x(0)
            with dve.Fori(0, TILES // RING) as lap:
                for i in range(RING):
                    t = RING * lap + i
                    split_low(W_all[1], w2, expert(t), w2_high, w2_low, t)
                    for f in range(KT):
                        dve.wait_ge(h_high, KT * t + (f + 1))
                        dve.tensor_tensor(hT[1][:, f], h[:, f], hT[0][:, f].bitcast(F32), ALU.subtract).then_inc(h_low, 1)
                    split_low(W_all[0], w1, expert(t + 1), w1_high, w1_low, t + 1)
                    low_of_x(t + 1)
                    for r in range(R):
                        dve.wait_ge(resid_ready, R * t + (R * RING + r + 1))
                        dve.wait_ge(y_full, R * t + (R + r + 1))
                        dve.scalar_tensor_tensor(out=rows[:, i, r], in0=py[:, r], scalar=cur[:, i, r, 1:2],
                                                 in1=rows[:, i, r], op0=ALU.mult, op1=ALU.add).then_inc(y_taken, 1)

        @block.tensor
        def _(pe):
            pe.sem_inc(g_logits, 2)
            pe.wait_ge(const_step, N_CONST)
            pe.wait_ge(const_loaded, 32)
            pe.wait_ge(wg_loaded, 16)
            pe.transpose(py[:, 0, 0:E * KT], b1_rows, ident[0:E * KT, 0:E * KT]).then_inc(b1_full, 1)

            def gate(b, half, t):
                if t == 0:
                    pe.wait_ge(g_taken, b + 1)
                pe.wait_ge(g_copied, NB * b + (t + 3))
                for k in range(KT):
                    op = pe.matmul(lg[half][:, t], gxT[t % 2][:, k * P:(k + 1) * P], wg[:, k],
                                   start=k == 0, stop=k == KT - 1)
                op.then_inc(g_logits, 1)

            with pe.Fori(0, B // 2) as pair:
                for half in range(2):
                    b = 2 * pair + half
                    for t in range(NB):
                        pe.wait_ge(g_norm, NB * b + (t + 1))
                        pe.wait_ge(g_copied, NB * b + (t + 1))
                        for k in range(KT):
                            op = pe.transpose(pT[:, t % 2, k * P:(k + 1) * P], gx[half][:, t, k * P:(k + 1) * P], ident[:])
                        op.then_inc(g_full, 1)
                        if t >= 1:
                            gate(b, half, t - 1)
                    gate(b, half, NB - 1)
            pe.wait_ge(hot_ready, 1)
            pe.matmul(rank.rearrange("p t e -> p (t e)"), earlier, hot.rearrange("p t e -> p (t e)"), start=True, stop=True)
            pe.matmul(totals.rearrange("p t e -> p (t e)"), ones, hot.rearrange("p t e -> p (t e)"), start=True, stop=True).then_inc(ranked, 1)

            def transposes(t):
                for r in range(R):
                    pe.wait_ge(normed, R * t + (r + 1))
                    for k in range(KT):
                        op = pe.transpose(pT[:, r, k * P:(k + 1) * P], xn[:, r, k * P:(k + 1) * P], ident[:])
                    op.then_inc(t_full, 1)

            transposes(0)
            with pe.Fori(0, TILES // RING) as lap:
                for i in range(RING):
                    t = RING * lap + i
                    pe.wait_ge(xT_low, R * t + R)
                    for f in range(KT):
                        for k in range(KT):
                            if f == 0 and k % KC == 0:
                                pe.wait_ge(w1_low, CH * t + (k // KC + 1))
                            for n, (x, y) in enumerate(SPLIT):
                                op = pe.matmul(ph[:, f], w1[x][:, k, f * P:(f + 1) * P], xT[y][:, k],
                                               start=k == 0 and n == 0, stop=k == KT - 1 and n == len(SPLIT) - 1)
                        op.then_inc(h_full, 1)
                    transposes(t + 1)
                    pe.wait_ge(y_taken, R * t + R)
                    for k in range(KT):
                        if k % KC == 0:
                            pe.wait_ge(w2_low, CH * t + (k // KC + 1))
                        pe.wait_ge(h_low, KT * t + (k + 1))
                        for r in range(R):
                            for n, (x, y) in enumerate(SPLIT):
                                op = pe.matmul(py[:, r], hT[x][:, k, r * P:(r + 1) * P], w2[y][:, k],
                                               start=k == 0 and n == 0, stop=k == KT - 1 and n == len(SPLIT) - 1)
                            if k == KT - 1:
                                op.then_inc(y_full, 1)


def decoder_layer(nc, x, ctx_1024, mask, w_qkv, b_qkv, w_dense, b_dense, Wq, bq, Wk, bk, Wv, bv, Wo, bo_x,
                  Wg, bg, W1, b1, W2, b2, out):
    x1 = nc.dram_tensor("x_after_self", (B, S, D), F32).ap()
    x2 = nc.dram_tensor("x_after_cross", (B, S, D), F32).ap()
    scratch_mask = nc.dram_tensor("mask_rows", (B, S), F32).ap()

    def self_weights():
        def part(k):
            return (w_qkv[k * P:(k + 1) * P, :],
                    lambda w: w[:, k, 0:3].rearrange("p s (h d) -> p s h d", d=HD),
                    lambda raw: raw[:, 0:3 * D].rearrange("p (h s d) -> p s h d", s=3, d=HD))
        dense = (w_dense.rearrange("(t p) d -> p t d", p=P), lambda w: w[:, :, 3],
                 lambda raw: raw.rearrange("p (t d) -> p t d", d=D))
        return [part(k) for k in range(KT)] + [dense]

    def self_biases(nc, sp, bias, loaded):
        cols = b_qkv.rearrange("(g j s d) -> j s d g", g=G, j=J, s=3)
        with nc.allow_non_contiguous_dma("a few hundred biases, once"):
            for j in range(J):
                for s in range(3):
                    sp.dma_start(bias[HD * j:HD * (j + 1), s], cols[j, s]).then_inc(loaded, 16)

    def cross_weights():
        def part(s, w_in):
            return (w_in.rearrange("(t p) d -> p t d", p=P), lambda w: w[:, :, s],
                    lambda raw: raw.rearrange("p (t d) -> p t d", d=D))
        return [part(s, w) for s, w in enumerate((Wq, Wk, Wv, Wo))]

    def cross_biases(nc, sp, bias, loaded):
        with nc.allow_non_contiguous_dma("a few hundred biases, once"):
            for s, v in enumerate((bq, bk, bv)):
                sp.dma_start(bias[:, s], v.rearrange("(g p) -> p g", p=P)).then_inc(loaded, 16)

    attention_layer(nc, "self", True, x, x1, None, None, None, self_weights, self_biases, b_dense)
    attention_layer(nc, "cross", False, x1, x2, ctx_1024, mask, scratch_mask, cross_weights, cross_biases, bo_x)
    expert_layer(nc, x2, out, Wg, bg, W1, b1, W2, b2)


_INS = ["x", "ctx_1024", "mask_BxS2_bk0",
        "L0_attn_w_qkv", "L0_attn_b_qkv", "L0_attn_w_dense", "L0_attn_b_dense",
        "L0_xattn_Wq", "L0_xattn_bq", "L0_xattn_Wk", "L0_xattn_bk", "L0_xattn_Wv", "L0_xattn_bv",
        "L0_xattn_Wo", "L0_xattn_bo",
        "L0_ffn_Wg", "L0_ffn_bg", "L0_ffn_W1", "L0_ffn_b1", "L0_ffn_W2", "L0_ffn_b2"]


def kernel(**inputs):
    import numpy as _np
    import concourse.bacc as _bacc
    from concourse import mybir as _mybir
    from concourse.bass_utils import run_bass_kernel_spmd as _run

    nc = _bacc.Bacc("TRN2", target_bir_lowering=False, num_devices=1)
    arrays, args = {}, []
    for name in _INS:
        a = _np.ascontiguousarray(inputs[name])
        if a.dtype == _np.bool_:
            a = a.view(_np.int32)
        arrays[f"in_{name}_dram"] = a
        args.append(nc.dram_tensor(f"in_{name}_dram", a.shape, _mybir.dt.from_np(a.dtype), kind="ExternalInput").ap())
    args.append(nc.dram_tensor("out_0_dram", (B, S, D), _mybir.dt.float32, kind="ExternalOutput").ap())
    decoder_layer(nc, *args)
    r = _run(nc, [arrays], core_ids=[0])
    return r.results[0]["out_0_dram"]
```

```python
import concourse.bass as bass
from concourse import mybir
from contextlib import ExitStack

ALU = mybir.AluOpType
ACT = mybir.ActivationFunctionType
AX_X = mybir.AxisListType.X
F32 = mybir.dt.float32
F32R = mybir.dt.float32r
BF16 = mybir.dt.bfloat16
I32 = mybir.dt.int32
U8 = mybir.dt.uint8

P = 128
B, S, D = 8, 512, 512
H, HD = 16, 32
KT = D // P
NB = S // P
G, J = 4, 4
N_EXPERT = 8
EPS = 1e-5
LOWEST = -(2.0 ** 100)
SCALE = float(HD) ** -0.5
ROW_MASK, ROW_MAX = 96, 97
SPLIT = ((0, 0), (0, 1), (1, 0))


def attention_layer(nc, name, causal, x_in, x_out, ctx_in, mask_in, scratch_mask,
                    load_weights, load_biases, b_out):
    cross = ctx_in is not None
    order = [("q", 0), ("k", 0), ("q", 1), ("k", 1), ("v", 0), ("v", 1), ("q", 2), ("k", 2), ("q", 3), ("k", 3),
             ("v", 2), ("v", 3), ("mT", 1)]
    order += [("mT", 2), ("bc", 0), ("mT", 3), ("bc", 1), ("bc", 2)] + [("wo", t) for t in range(NB)]
    FIRST = 2
    N_ITEM = len(order)
    at = {key: i for i, key in enumerate(order)}
    his = [key for key in order if key[0] in ("q", "k")]
    N_HI = len(his)
    hi_at = {key: i for i, key in enumerate(his)}
    N_STACK, N_STACK_POOL = 3 * (J - 1) + (1 if cross else 0), 3
    later = [(g, n) for g in range(1, G) for n in range(J * NB)]

    def beside(step):
        return later[J * step:J * (step + 1)]

    with ExitStack() as ctx:
        def sb(nm, shape, dt=F32):
            return ctx.enter_context(nc.sbuf_tensor(f"{name}_{nm}", shape, dt))

        def ps(nm, shape):
            return ctx.enter_context(nc.psum_tensor(f"{name}_{nm}", shape, F32))

        def sem(nm):
            return ctx.enter_context(nc.semaphore(f"{name}_{nm}"))

        W = [sb("w_high", [P, KT, 4, D], F32R), sb("w_low", [P, KT, 4, D], F32R)]
        stack = sb("stack", [P, G, 2, J, S], F32R)
        xT = [sb("xT_high", [P, KT, S], F32R), sb("xT_low", [P, KT, S], F32R)]
        oT = [sb("oT_high", [P, KT, S], F32R), sb("oT_low", [P, KT, S], F32R)]
        kvT = oT if cross else xT
        V = sb("V", [P, NB, D])
        probs = sb("probs", [P, 2, J, S])
        stage = sb("stage", [P, 4, S], F32R)
        xb = sb("xb", [P, NB, D])
        o_sb = sb("o_sb", [P, S])
        bo = sb("bo", [P, D])
        ident = sb("ident", [P, P])
        onehot = sb("onehot", [P, HD + NB - 1])
        m_neg = sb("m_neg", [J * NB, P], F32R)
        m_col = sb("m_col", [P, 2, J * NB])
        rec = sb("rec", [P, P])
        bias = sb("bias", [P, 3, G])
        stats = sb("stats", [P, NB, 6])
        mv = sb("mv", [P, NB, 2])
        ln_const = sb("ln_const", [P, 3, NB])
        rstd = sb("rstd", [P, NB])
        nmr = sb("nmr", [P, NB])
        if not cross:
            tri = sb("tri", [P, 2 * S - P], BF16)

        pj = ps("pj", [P, 2, S])
        sS = ps("sS", [P, 2, S])
        sT = ps("sT", [P, 2, S])
        o_ps = ps("o_ps", [P, S])
        den = ps("den", [P, S])

        raw_loaded = [sem(f"raw_loaded_{i}") for i in range(3)]
        raw_high, raw_done = sem("raw_high"), sem("raw_done")
        const_loaded, const_step = sem("const_loaded"), sem("const_step")
        if cross:
            mask_loaded, mask_ready, mask_stored = sem("mask_loaded"), sem("mask_ready"), sem("mask_stored")
            ctx_loaded = sem("ctx_loaded")
            tc_full, tc_high, tc_low = sem("tc_full"), sem("tc_high"), sem("tc_low")
        else:
            masked = sem("masked")
        x_loaded, resid_loaded = sem("x_loaded"), sem("resid_loaded")
        stacked = [sem("stacked_even"), sem("stacked_odd")]
        stacked_last = [sem("stacked_last_even"), sem("stacked_last_odd")]
        max_stacked, stored = sem("max_stacked"), sem("stored")
        first_max, first_max_taken = sem("first_max"), sem("first_max_taken")
        last_rec, last_rec_taken = sem("last_rec"), sem("last_rec_taken")
        ln_stats, ln_step, ln_ready, xn_ready = sem("ln_stats"), sem("ln_step"), sem("ln_ready"), sem("xn_ready")
        dve_step = sem("dve_step")
        waited = sem("waited")
        pj_full, pj_free, high_done = sem("pj_full"), sem("pj_free"), sem("high_done")
        tx_full, tx_high, tx_low = sem("tx_full"), sem("tx_high"), sem("tx_low")
        s_full, s_free = sem("s_full"), sem("s_free")
        st_full, exp_done, pv_done = sem("st_full"), sem("exp_done"), sem("pv_done")
        o_copied, rec_ready, oT_high, oT_ready = sem("o_copied"), sem("rec_ready"), sem("oT_high"), sem("oT_ready")
        resid_ready = sem("resid_ready")

        def filled(b, key):
            return N_ITEM * b + (at[key] + 1)

        def bank_free(b, key):
            return N_ITEM * b + (at[key] + 1)

        def wait_stacked(eng, b, g):
            eng.wait_ge(stacked[g % 2], 16 * N_STACK * 2 * b + 16 * N_STACK * (g // 2 + 1))
            eng.wait_ge(stacked_last[g % 2], 16 * N_STACK_POOL * 2 * b + 16 * N_STACK_POOL * (g // 2 + 1))

        def taken(b, key):
            return N_ITEM * b + (at[key] + 3)

        stage_f32, stack_f32 = stage[:].bitcast(F32), stack[:].bitcast(F32)
        split_qk = [stage[:], xb[:].bitcast(F32R)]
        split_f32 = [stage_f32, xb[:]]
        x_rows = x_in.rearrange("b (t p) d -> b p t d", p=P)
        out_rows = x_out.rearrange("b (t p) d -> b p t d", p=P)
        ctx_rows = ctx_in.rearrange("b (t p) d -> b p t d", p=P) if cross else None
        weights = load_weights()
        raw_buffers = [probs[:, 1].rearrange("p j s -> p (j s)"), V[:].rearrange("p t d -> p (t d)"),
                       probs[:, 0].rearrange("p j s -> p (j s)")]
        mask_f32 = o_sb[0:B, :]
        mask_u8 = rec[0:B, 0:S // 4].bitcast(U8)
        N_CONST = 4 if cross else 13
        N_STEP = 8 if cross else 11
        PV0 = G * NB
        block = ctx.enter_context(nc.Block())

        def weight_views(i):
            src, to, of = weights[i]
            raw = raw_buffers[i % 3]
            return src, raw, [to(W[h]) for h in range(2)], of(raw)

        def raw_dst(raw, src):
            n = 1
            for s in src.shape[1:]:
                n *= s
            r = raw[:, 0:n]
            return r if len(src.shape) == 2 else r.rearrange("p (t d) -> p t d", t=src.shape[1])

        def stack_head(eng, g, j, done):
            of, rows = split_f32[g % 2], slice(HD * j, HD * (j + 1))
            eng.dma_start(stack_f32[0:HD, g, :, j], of[rows, 1:3]).then_inc(done, 16)
            eng.dma_start(stack_f32[HD:2 * HD, g, :, j], of[rows, 0:3:2]).then_inc(done, 16)
            eng.dma_start(stack_f32[2 * HD:3 * HD, g, :, j], of[rows, 1:4:2]).then_inc(done, 16)

        @block.sync
        def _(sp):
            sp.dma_start(xb[:], x_rows[0]).then_inc(x_loaded, 16)
            for i in range(len(weights)):
                if i >= 3:
                    sp.wait_ge(raw_done, i - 2)
                src, raw, _, _ = weight_views(i)
                sp.dma_start(raw_dst(raw, src), src).then_inc(raw_loaded[i % 3], 16)
            if cross:
                sp.wait_ge(raw_done, 3)
                sp.dma_start(probs[:, 0], ctx_rows[0]).then_inc(ctx_loaded, 16)
                sp.wait_ge(mask_stored, 16)

            def stack_group(b, g):
                sp.wait_ge(pj_free, taken(b, ("k", g)))
                sp.sem_inc(waited, 1)
                sp.wait_ge(pv_done, PV0 * b + NB * (g + 1))
                for j in range(J - 1):
                    stack_head(sp, g, j, stacked[g % 2])
                if cross:
                    sp.dma_start(stack_f32[ROW_MASK:ROW_MASK + 1, g, 1],
                                 scratch_mask[bass.ds(b, 1)].unsqueeze(1).broadcast_to([1, J, S])).then_inc(stacked[g % 2], 16)

            def stack_max(b, g):
                if g == 0:
                    sp.wait_ge(first_max_taken, b + 1)
                else:
                    sp.wait_ge(pj_free, taken(b, ("mT", g)))
                sp.dma_start(stack_f32[ROW_MAX:ROW_MAX + 1, g, 0].rearrange("o j s -> o (j s)"),
                             m_neg[:].bitcast(F32)).then_inc(max_stacked, 16)

            with sp.Fori(0, B) as b:
                nxt = sp.snap((b + 1) % B)
                for g in range(G - 1):
                    stack_group(b, g)
                stack_max(b, 0)
                stack_group(b, G - 1)
                wait_stacked(sp, b, 2)
                sp.sem_inc(waited, 1)
                sp.dma_start(stage_f32, x_rows[b]).then_inc(resid_loaded, 16)
                wait_stacked(sp, b, 3)
                sp.sem_inc(waited, 1)
                sp.dma_start(xb[:], x_rows[nxt]).then_inc(x_loaded, 16)
                for g in range(1, G):
                    stack_max(b, g)
                if cross:
                    sp.wait_ge(pv_done, PV0 * b + (PV0 + PV0 - 1))
                    sp.sem_inc(waited, 1)
                    sp.dma_start(probs[:, 0], ctx_rows[nxt]).then_inc(ctx_loaded, 16)
                for t in range(NB):
                    sp.wait_ge(pj_free, taken(b, ("wo", t)))
                    sp.sem_inc(waited, 1)
                    sp.dma_start(out_rows[b][:, t], stage_f32[:, t]).then_inc(stored, 16)
            sp.wait_ge(stored, 16 + 16 * NB * B)
            if cross:
                sp.wait_ge(ctx_loaded, 16 * (B + 1))

        @block.gpsimd
        def _(pool):
            pool.sem_inc(pj_free, 2)
            pool.sem_inc(s_free, 2)
            pool.sem_inc(exp_done, 2)
            pool.sem_inc(pv_done, PV0)
            pool.sem_inc(o_copied, 1)
            pool.sem_inc(rec_ready, 1)
            pool.sem_inc(oT_ready, 1)
            pool.sem_inc(stored, 16)
            pool.memset(ident[:], 0.0).then_inc(const_step, 1)
            pool.memset(onehot[:], 0.0).then_inc(const_step, 1)
            for n, value in enumerate((EPS, -0.5, -1.0)):
                pool.memset(ln_const[:, n], value).then_inc(const_step, 1)
            pool.wait_ge(const_step, 5)
            pool.affine_select(out=ident[:], in_=ident[:], compare_op=ALU.not_equal, fill=1.0, base=0,
                               pattern=[[-1, P]], channel_multiplier=1).then_inc(const_step, 1)
            pool.memset(onehot[:, NB - 1::NB], 1.0).then_inc(const_step, 1)
            if cross:
                pool.dma_start(mask_u8.bitcast(I32), mask_in).then_inc(mask_loaded, 16)

            def layernorm_scale(b):
                pool.wait_ge(ln_stats, b + 1)
                pool.tensor_tensor(rstd[:], mv[:, :, 1], ln_const[:, 0], ALU.add).then_inc(ln_step, 1)
                pool.wait_ge(ln_step, 3 * b + 1)
                pool.tensor_tensor(rstd[:], rstd[:], ln_const[:, 1], ALU.pow).then_inc(ln_step, 1)
                pool.wait_ge(ln_step, 3 * b + 2)
                pool.tensor_tensor(nmr[:], mv[:, :, 0], rstd[:], ALU.mult).then_inc(ln_step, 1)
                pool.wait_ge(ln_step, 3 * b + 3)
                pool.tensor_tensor(nmr[:], nmr[:], ln_const[:, 2], ALU.mult).then_inc(ln_ready, 1)

            layernorm_scale(0)
            pool.wait_ge(ln_ready, 1)
            pool.memset(stack_f32[ROW_MASK:ROW_MAX + 1], 1.0).then_inc(const_step, 1)
            if not cross:
                pool.wait_ge(const_step, 8)
                pool.memset(stack_f32[ROW_MASK:ROW_MASK + 1, :, 1], 0.0).then_inc(const_step, 1)
                pool.wait_ge(const_step, 9)
                pool.memset(tri[:], 0.0).then_inc(const_step, 1)
                pool.wait_ge(const_step, 10)
                pool.affine_select(out=tri[:], in_=tri[:], compare_op=ALU.is_ge, fill=LOWEST, base=S - P,
                                   pattern=[[-1, 2 * S - P]], channel_multiplier=1).then_inc(const_step, 1)
            else:
                pool.wait_ge(const_step, 8)
                pool.wait_ge(mask_loaded, 16)
                pool.tensor_scalar(mask_f32, mask_u8, LOWEST, None, ALU.mult).then_inc(mask_ready, 1)
                pool.wait_ge(mask_ready, 1)
                pool.dma_start(scratch_mask, mask_f32).then_inc(mask_stored, 16)
            def stack_last_head(b, g):
                pool.wait_ge(pj_free, taken(b, ("k", g)))
                pool.sem_inc(waited, 1)
                pool.wait_ge(pv_done, PV0 * b + NB * (g + 1))
                pool.sem_inc(waited, 1)
                stack_head(pool, g, J - 1, stacked_last[g % 2])

            with pool.Fori(0, B) as b:
                for g in range(G):
                    stack_last_head(b, g)
                for g in range(G):
                    for kb in range(NB):
                        if not cross:
                            pool.wait_ge(exp_done, G * NB * J * b + (2 + (g * NB + kb + 1) * J))
                            pool.sem_inc(waited, 1)
                            diag = probs[:, kb % 2, :, kb * P:(kb + 1) * P]
                            pool.affine_select(out=diag, in_=diag, compare_op=ALU.is_ge, fill=0.0, base=0,
                                               pattern=[[0, J], [1, P]], channel_multiplier=-1).then_inc(masked, 1)
                        if g == 1:
                            if kb == 0:
                                pool.wait_ge(resid_loaded, 16 * b + 16)
                                pool.sem_inc(waited, 1)
                            pool.tensor_tensor(stage_f32[:, kb], stage_f32[:, kb], bo[:], ALU.add).then_inc(resid_ready, 1)
                        if g == 2 and kb == 0:
                            layernorm_scale(b + 1)

        @block.scalar
        def _(act):
            load_biases(nc, act, bias, const_loaded)
            act.dma_start(bo[:], b_out.partition_broadcast(P)).then_inc(const_loaded, 16)

            def high_of_weights(i):
                act.wait_ge(raw_loaded[i % 3], 16 * (i // 3 + 1))
                _, _, (high, _), raw = weight_views(i)
                act.copy(high, raw).then_inc(raw_high, 1)

            def normalize(b, t):
                act.wait_ge(ln_ready, b + 1)
                act.activation(xb[:, t], xb[:, t], ACT.Identity, scale=rstd[:, t:t + 1],
                               bias=nmr[:, t:t + 1]).then_inc(xn_ready, 1)

            def high_of_rows(b, t):
                act.wait_ge(tx_full, NB * b + (t + 1))
                act.copy(xT[0][:, :, t * P:(t + 1) * P],
                         sS[:, t % 2].rearrange("p (k s) -> p k s", k=KT)).then_inc(tx_high, 1)

            def high_of_context(b, t):
                act.wait_ge(tc_full, NB * b + (t + 1))
                act.copy(oT[0][:, :, t * P:(t + 1) * P],
                         (sS, sT)[t // 2][:, t % 2].rearrange("p (k s) -> p k s", k=KT)).then_inc(tc_high, 1)

            def high_of_qk(b, which, g):
                if which == 0 and g == 0:
                    act.wait_ge(stored, 16 * NB * b + 16)
                elif which == 0 and g >= 2:
                    wait_stacked(act, b, g - 2)
                i = at["qk"[which], g]
                act.wait_ge(pj_full, filled(b, ("qk"[which], g)))
                act.activation(split_qk[g % 2][:, 1 + which], pj[:, i % 2], ACT.Identity,
                               bias=bias[:, which, g:g + 1]).then_inc(high_done, 1)

            def attend(b, g):
                for kb in range(NB):
                    q0 = kb * P if not cross else 0
                    act.wait_ge(pv_done, PV0 * b + (PV0 + g * NB + kb - 1))
                    for j in range(J):
                        n = (g * NB + kb) * J + j
                        act.wait_ge(st_full, G * NB * J * b + (n + 1))
                        act.activation(probs[:, kb % 2, j, q0:S], sT[:, n % 2, q0:S], ACT.Exp,
                                       scale=SCALE).then_inc(exp_done, 1)
                    if kb == 0 and g >= 1:
                        copy_output(b, g - 1)
                    if kb == 2 and g >= 1:
                        high_of_output(b, g - 1)
                    if g == 2 and kb >= 1:
                        normalize(b + 1, kb - 1)
                    if g == 2 and kb == NB - 1:
                        normalize(b + 1, kb)
                    if g == 3 and kb >= 1:
                        high_of_rows(b + 1, kb - 1)

            def copy_output(b, g):
                act.wait_ge(oT_ready, G * b + (g + 1))
                act.wait_ge(pv_done, PV0 * b + (PV0 + (g + 1) * NB))
                act.copy(o_sb[:], o_ps[:]).then_inc(o_copied, 1)

            def high_of_output(b, g):
                if g == G - 1:
                    act.wait_ge(last_rec_taken, b + 1)
                else:
                    act.wait_ge(pj_free, taken(b, ("bc", g)))
                act.activation(oT[0][:, g], o_sb[:], ACT.Identity, bias=bias[:, 2, g:g + 1]).then_inc(oT_high, 1)

            high_of_weights(0)
            for t in range(NB):
                normalize(0, t)
            high_of_weights(1)
            for t in range(NB):
                high_of_rows(0, t)
            for i in range(2, len(weights)):
                high_of_weights(i)
            act.wait_ge(const_loaded, 16 * N_CONST)
            with act.Fori(0, B) as b:
                if cross:
                    for t in range(NB):
                        high_of_context(b, t)
                for g in range(G):
                    for which in range(2):
                        high_of_qk(b, which, g)
                for g in range(G):
                    attend(b, g)
                copy_output(b, G - 1)
                high_of_rows(b + 1, NB - 1)
                high_of_output(b, G - 1)

        @block.vector
        def _(dve):
            def low_of_weights(i):
                dve.wait_ge(raw_high, i + 1)
                _, _, (high, low), raw = weight_views(i)
                dve.tensor_tensor(low, raw, high.bitcast(F32), ALU.subtract).then_inc(raw_done, 1)

            def row_stats(b, t):
                if t == 0:
                    dve.wait_ge(x_loaded, 16 * b + 16)
                    dve.sem_inc(waited, 1)
                dve.bn_stats(stats[:, t], xb[:, t]).then_inc(dve_step, 1)

            def mean_and_variance(b):
                for t in range(NB):
                    dve.wait_ge(dve_step, NB * b + (t + 1))
                    dve.sem_inc(waited, 1)
                    last = dve.bn_aggr(mv[:, t], stats[:, t])
                last.then_inc(ln_stats, 1)

            def low_of_rows(b, t):
                dve.wait_ge(tx_high, NB * b + (t + 1))
                cols = slice(t * P, (t + 1) * P)
                dve.tensor_tensor(xT[1][:, :, cols], sS[:, t % 2].rearrange("p (k s) -> p k s", k=KT),
                                  xT[0][:, :, cols].bitcast(F32), ALU.subtract).then_inc(tx_low, 1)

            def low_of_context(b, t):
                dve.wait_ge(tc_high, NB * b + (t + 1))
                cols = slice(t * P, (t + 1) * P)
                dve.tensor_tensor(oT[1][:, :, cols], (sS, sT)[t // 2][:, t % 2].rearrange("p (k s) -> p k s", k=KT),
                                  oT[0][:, :, cols].bitcast(F32), ALU.subtract).then_inc(tc_low, 1)

            def low_of_qk(b, which, g):
                i = at["qk"[which], g]
                dve.wait_ge(high_done, N_HI * b + (hi_at["qk"[which], g] + 1))
                op = dve.scalar_tensor_tensor(out=split_qk[g % 2][:, 3 * which], in0=pj[:, i % 2], scalar=bias[:, which, g:g + 1],
                                              in1=split_f32[g % 2][:, 1 + which], op0=ALU.add, op1=ALU.subtract)
                op.then_inc(pj_free, 1)

            def copy_v(b, t):
                i = at["v", t]
                dve.wait_ge(pj_full, N_ITEM * b + (i + 1))
                dve.tensor_copy(V[:, t], pj[:, i % 2]).then_inc(pj_free, 1)

            def maxima(b, blocks):
                for g, n in blocks:
                    j, qb = n // NB, n % NB
                    m = g * J * NB + n
                    dve.wait_ge(s_full, G * J * NB * b + (m + 1))
                    to = m_col[:, g % 2, n:n + 1]
                    if cross:
                        op = dve.tensor_reduce(to, sS[:, m % 2], AX_X, ALU.max)
                    else:
                        width = (qb + 1) * P
                        dve.sem_inc(waited, 1)
                        op = dve.tensor_tensor_reduce(sS[:, m % 2, 0:width], sS[:, m % 2, 0:width],
                                                      tri[:, S - P - qb * P:S - P - qb * P + width],
                                                      1.0, LOWEST, ALU.add, ALU.max, to)
                    op.then_inc(s_free, 1)

            def negate_max(b, g):
                if g == 0:
                    dve.wait_ge(first_max, b + 1)
                    dve.tensor_scalar(m_neg[:], sT[0:J * NB, 0, 0:P], -1.0, None, ALU.mult).then_inc(first_max_taken, 1)
                else:
                    i = at["mT", g]
                    dve.wait_ge(pj_full, filled(b, ("mT", g)))
                    dve.tensor_scalar(m_neg[:], pj[0:J * NB, i % 2, 0:P], -1.0, None, ALU.mult).then_inc(pj_free, 1)

            def reciprocals(b, g):
                dve.wait_ge(pv_done, PV0 * b + (PV0 + (g + 1) * NB))
                dve.reciprocal(rec[:], den[:, 0:P]).then_inc(rec_ready, 1)

            def divide(b, g):
                dve.wait_ge(o_copied, G * b + (g + 2))
                if g == G - 1:
                    dve.wait_ge(last_rec, b + 1)
                    dve.tensor_tensor(o_sb[:], sT[:, 0], o_sb[:], ALU.mult).then_inc(last_rec_taken, 1)
                else:
                    i = at["bc", g]
                    dve.wait_ge(pj_full, filled(b, ("bc", g)))
                    dve.tensor_tensor(o_sb[:], pj[:, i % 2], o_sb[:], ALU.mult).then_inc(pj_free, 1)

            def low_of_output(b, g):
                dve.wait_ge(oT_high, G * b + (g + 1))
                dve.scalar_tensor_tensor(out=oT[1][:, g], in0=o_sb[:], scalar=bias[:, 2, g:g + 1],
                                         in1=oT[0][:, g].bitcast(F32), op0=ALU.add, op1=ALU.subtract).then_inc(oT_ready, 1)

            def add_rows(b, t):
                i = at["wo", t]
                dve.wait_ge(resid_ready, NB * b + (t + 1))
                dve.wait_ge(pj_full, N_ITEM * b + (i + 1))
                dve.tensor_tensor(stage_f32[:, t], pj[:, i % 2], stage_f32[:, t], ALU.add).then_inc(pj_free, 1)

            for t in range(NB):
                row_stats(0, t)
            mean_and_variance(0)
            low_of_weights(0)
            low_of_weights(1)
            for t in range(NB):
                low_of_rows(0, t)
            for i in range(2, len(weights)):
                low_of_weights(i)
            dve.wait_ge(const_loaded, 16 * N_CONST)
            with dve.Fori(0, B) as b:
                if cross:
                    for t in range(NB):
                        low_of_context(b, t)
                for g in range(2):
                    for which in range(2):
                        low_of_qk(b, which, g)
                copy_v(b, 0)
                copy_v(b, 1)
                dve.wait_ge(const_step, N_STEP)
                for n, (which, g) in enumerate([(0, 2), (1, 2), (0, 3), (1, 3)]):
                    maxima(b, [(0, n * NB + k) for k in range(NB)])
                    low_of_qk(b, which, g)
                maxima(b, beside(0))
                copy_v(b, 2)
                negate_max(b, 0)
                maxima(b, beside(1))
                copy_v(b, 3)
                maxima(b, beside(2))
                for g in range(G):
                    for kb in range(NB):
                        blocks = beside(3 + g * NB + kb)
                        if kb == 1 and g + 1 < G:
                            negate_max(b, g + 1)
                        maxima(b, blocks[:2])
                        if kb == 0 and g >= 1:
                            reciprocals(b, g - 1)
                        maxima(b, blocks[2:])
                        if kb == 1 and g >= 1:
                            divide(b, g - 1)
                        if kb == 3 and g >= 1:
                            low_of_output(b, g - 1)
                        if g == 1:
                            row_stats(b + 1, kb)
                            if kb == NB - 1:
                                mean_and_variance(b + 1)
                        if g == 3 and kb >= 1:
                            low_of_rows(b + 1, kb - 1)
                reciprocals(b, G - 1)
                low_of_rows(b + 1, NB - 1)
                divide(b, G - 1)
                low_of_output(b, G - 1)
                for t in range(NB):
                    add_rows(b, t)

        @block.tensor
        def _(pe):
            def transposes(bank, rows, done):
                for k in range(KT):
                    op = pe.transpose(bank[:, k * P:(k + 1) * P], rows[:, k * P:(k + 1) * P], ident[:])
                op.then_inc(done, 1)

            def transposed_rows(b, t):
                pe.wait_ge(xn_ready, NB * b + (t + 1))
                pe.wait_ge(tx_low, NB * b + (t - 1))
                transposes(sS[:, t % 2], xb[:, t], tx_full)

            def split_product(out, a_of, b_of, start, stop, between=None):
                ops = None
                for k in range(KT):
                    for n, (x, y) in enumerate(SPLIT):
                        ops = pe.matmul(out, a_of(x, k), b_of(y, k), start=start and k == 0 and n == 0,
                                        stop=stop and k == KT - 1 and n == len(SPLIT) - 1)
                    if between is not None:
                        between(k)
                return ops

            def project_qk(b, which, g, between=None):
                i = at["qk"[which], g]
                pe.wait_ge(pj_free, N_ITEM * b + (i + 1))
                src = xT if which == 0 else kvT
                split_product(pj[:, i % 2], lambda x, k: W[x][:, k, which, g * P:(g + 1) * P],
                              lambda y, k: src[y][:, k], True, True, between).then_inc(pj_full, 1)

            def project_v(b, t, between=None):
                i = at["v", t]
                pe.wait_ge(pj_free, N_ITEM * b + (i + 1))
                split_product(pj[:, i % 2], lambda x, k: kvT[x][:, k, t * P:(t + 1) * P],
                              lambda y, k: W[y][:, k, 2], True, True, between).then_inc(pj_full, 1)

            def scores(b, g, n):
                j, qb = n // NB, n % NB
                m = g * J * NB + n
                width = S if cross else max((qb + 1) * P, 2 * P)
                pe.wait_ge(s_free, G * J * NB * b + (m + 1))
                pe.matmul(sS[:, m % 2, 0:width], stack[0:ROW_MAX, g, 0, j, qb * P:(qb + 1) * P],
                          stack[0:ROW_MAX, g, 1, j, 0:width], start=True, stop=True).then_inc(s_full, 1)

            def max_rows(b, g):
                pe.wait_ge(s_free, G * J * NB * b + (2 + (g + 1) * J * NB))
                if g == 0:
                    pe.transpose(sT[0:J * NB, 0, 0:P], m_col[:, g % 2], ident[:]).then_inc(first_max, 1)
                else:
                    i = at["mT", g]
                    pe.wait_ge(pj_free, N_ITEM * b + (i + 1))
                    pe.transpose(pj[0:J * NB, i % 2, 0:P], m_col[:, g % 2], ident[:]).then_inc(pj_full, 1)

            def scores_T(b, g, kb, j):
                q0 = min(kb * P, S - 2 * P) if not cross else 0
                n = (g * NB + kb) * J + j
                pe.wait_ge(exp_done, G * NB * J * b + (n + 1))
                pe.matmul(sT[:, n % 2, q0:S], stack[0:ROW_MAX + 1, g, 1, j, kb * P:(kb + 1) * P],
                          stack[0:ROW_MAX + 1, g, 0, j, q0:S], start=True, stop=True).then_inc(st_full, 1)

            def weighted_values(b, g, kb):
                q0 = kb * P if not cross else 0
                if kb == 0:
                    pe.wait_ge(o_copied, G * b + (g + 1))
                pe.wait_ge(exp_done, G * NB * J * b + (2 + (g * NB + kb + 1) * J))
                if not cross:
                    pe.wait_ge(masked, G * NB * b + (g * NB + kb + 1))
                for j in range(J):
                    cols = slice((g * J + j) * HD, (g * J + j + 1) * HD)
                    pe.matmul(o_ps[HD * j:HD * (j + 1), q0:S], V[:, kb, cols], probs[:, kb % 2, j, q0:S],
                              start=kb == 0, stop=kb == NB - 1)

            def sums(b, g, kb):
                q0 = kb * P if not cross else 0
                if kb == 0:
                    pe.wait_ge(rec_ready, G * b + (g + 1))
                for qb in range(q0 // P, NB):
                    pick = onehot[:, NB - 1 - qb:NB - 1 - qb + HD]
                    for j in range(J):
                        op = pe.matmul(den[HD * j:HD * (j + 1), 0:P], pick, probs[:, kb % 2, j, qb * P:(qb + 1) * P],
                                       start=kb == 0 and qb == 0, stop=kb == NB - 1 and qb == NB - 1)
                op.then_inc(pv_done, 1)

            def spread_reciprocals(b, g):
                pe.wait_ge(rec_ready, G * b + (g + 2))
                if g == G - 1:
                    bank = sT[:, 0]
                else:
                    i = at["bc", g]
                    pe.wait_ge(pj_free, N_ITEM * b + (i + 1))
                    bank = pj[:, i % 2]
                for qb in range(NB):
                    for j in range(J):
                        pick = ident[:, HD * j + qb:HD * j + qb + 1].broadcast_to([P, HD])
                        op = pe.matmul(bank[HD * j:HD * (j + 1), qb * P:(qb + 1) * P], pick, rec[:],
                                       start=True, stop=True)
                op.then_inc(last_rec if g == G - 1 else pj_full, 1)

            def both_scores(b, step, g, kb, heads):
                for j in heads:
                    if g < G:
                        scores_T(b, g, kb, j)
                    if beside(step):
                        scores(b, *beside(step)[j])

            def attend(b, g):
                for kb in range(NB):
                    step = 3 + g * NB + kb
                    if kb == 1 and g + 1 < G:
                        max_rows(b, g + 1)
                    if kb == 1 and g >= 1:
                        spread_reciprocals(b, g - 1)
                    if kb == 1 and g + 2 < G:
                        wait_stacked(pe, b, g + 2)
                    if kb == 3 and g + 1 < G:
                        pe.wait_ge(max_stacked, 16 * G * b + 16 * (g + 2))
                    ahead = g + (kb + 1) // NB, (kb + 1) % NB
                    both_scores(b, step, *ahead, range(FIRST))
                    if g == 0 and kb == 0:
                        pe.wait_ge(pj_free, taken(b, ("v", 3)))
                    weighted_values(b, g, kb)
                    both_scores(b, step, *ahead, range(FIRST, J))
                    if g == G - 1:
                        transposed_rows(b + 1, kb)
                    sums(b, g, kb)

            def out_projection(b, t, gs):
                i = at["wo", t]
                for g in gs:
                    for n, (x, y) in enumerate(SPLIT):
                        op = pe.matmul(pj[:, i % 2], oT[x][:, g, t * P:(t + 1) * P], W[y][:, g, 3],
                                       start=g == 0 and n == 0, stop=g == G - 1 and n == len(SPLIT) - 1)
                if G - 1 in gs:
                    op.then_inc(pj_full, 1)

            pe.wait_ge(const_step, 7)
            for t in range(NB):
                pe.wait_ge(xn_ready, t + 1)
                if t >= 2:
                    pe.wait_ge(tx_low, t - 1)
                transposes(sS[:, t % 2], xb[:, t], tx_full)
            with pe.Fori(0, B) as b:
                pe.wait_ge(tx_low, NB * b + NB)
                if cross:
                    pe.wait_ge(ctx_loaded, 16 * b + 16)
                    for t in range(NB):
                        transposes((sS, sT)[t // 2][:, t % 2], probs[:, 0, t], tc_full)
                pe.wait_ge(raw_done, 1 if cross else KT)
                project_qk(b, 0, 0)
                pe.wait_ge(raw_done, 2 if cross else KT)
                if cross:
                    pe.wait_ge(tc_low, NB * b + NB)
                project_qk(b, 1, 0)
                project_qk(b, 0, 1)
                project_qk(b, 1, 1)
                pe.wait_ge(raw_done, 3 if cross else KT)
                project_v(b, 0)
                project_v(b, 1)
                wait_stacked(pe, b, 0)
                pe.wait_ge(const_step, N_STEP)
                for n, (which, g) in enumerate([(0, 2), (1, 2), (0, 3), (1, 3)]):
                    project_qk(b, which, g, lambda k, n=n: scores(b, 0, n * NB + k))
                wait_stacked(pe, b, 1)
                project_v(b, 2, lambda k: scores(b, *beside(0)[k]))
                max_rows(b, 0)
                project_v(b, 3, lambda k: scores(b, *beside(1)[k]))
                pe.wait_ge(max_stacked, 16 * G * b + 16)
                both_scores(b, 2, 0, 0, range(J))
                for g in range(G):
                    attend(b, g)
                pe.wait_ge(raw_done, len(weights))
                pe.wait_ge(oT_ready, G * b + G)
                for t in range(2):
                    pe.wait_ge(pj_free, bank_free(b, ("wo", t)))
                    out_projection(b, t, range(G - 1))
                    if t == 0:
                        spread_reciprocals(b, G - 1)
                pe.wait_ge(oT_ready, G * b + (G + 1))
                for t in range(2):
                    out_projection(b, t, range(G - 1, G))
                for t in range(2, NB):
                    pe.wait_ge(pj_free, bank_free(b, ("wo", t)))
                    out_projection(b, t, range(G))


def expert_layer(nc, x_in, x_out, Wg, bg, W1, b1, W2, b2):
    N = B * S
    NT = N // P
    E = N_EXPERT
    TOK = 2 * P
    R = TOK // P
    RING = 3
    TILES = (N + E * (TOK - 1)) // TOK
    LAPS, REST = TILES // RING, TILES % RING
    COLS = (TILES + RING) * R
    REC = 4
    NO_ROW = 2 * N
    SORT = 4
    CH = KT
    KC = KT // CH
    with ExitStack() as ctx:
        def sb(nm, shape, dt=F32):
            return ctx.enter_context(nc.sbuf_tensor(f"moe_{nm}", shape, dt))

        def ps(nm, shape):
            return ctx.enter_context(nc.psum_tensor(f"moe_{nm}", shape, F32))

        def sem(nm):
            return ctx.enter_context(nc.semaphore(f"moe_{nm}"))

        def sems(nm):
            return [sem(f"{nm}_{i}") for i in range(RING)]

        W_all = [sb("w1", [P, E, KT, D]), sb("w2", [P, E, KT, D])]
        w1 = [sb("w1_high", [P, KT, D], F32R), sb("w1_low", [P, KT, D], F32R)]
        w2 = [sb("w2_high", [P, KT, D], F32R), sb("w2_low", [P, KT, D], F32R)]
        rows = sb("rows", [P, RING, R, D])
        xn = sb("xn", [P, R, D])
        xT = [sb("xT_high", [P, KT, TOK], F32R), sb("xT_low", [P, KT, TOK], F32R)]
        h = sb("h", [P, KT, TOK])
        hT = [sb("hT_high", [P, KT, TOK], F32R), sb("hT_low", [P, KT, TOK], F32R)]
        b2_rows = sb("b2_rows", [P, RING, D])
        b1_cols = sb("b1_cols", [P, E, KT])
        rec_all = sb("rec_all", [P, COLS, REC])
        cur = sb("cur", [P, RING, R, REC])
        tile_expert = sb("tile_expert", [P, TILES + 1], I32)
        ident = sb("ident", [P, P])
        ln_const = sb("ln_const", [P, 3, NB])
        gx = [W_all[1][:, E - 2 + half] for half in range(2)]
        gxT = [W_all[1][:, E - 3, n] for n in range(2)]
        wg = xn[:, 0].rearrange("p (k c) -> p k c", k=KT)[:, :, 0:E]
        desk = rows[:].rearrange("p a r d -> p (a r d)")
        earlier, ones = desk[:, 0:P], desk[:, P:2 * P]
        stats = desk[:, 256:256 + 2 * NB * 6].rearrange("p (a t s) -> p a t s", a=2, t=NB)
        mv = desk[:, 320:320 + 2 * NB * 2].rearrange("p (a t s) -> p a t s", a=2, t=NB)
        rstd = desk[:, 352:352 + 2 * NB].rearrange("p (a t) -> p a t", a=2)
        nmr = desk[:, 376:376 + 2 * NB].rearrange("p (a t) -> p a t", a=2)
        rec_tok = b2_rows[:, 0, 0:NT * REC].rearrange("p (t r) -> p t r", t=NT)
        place_of = b2_rows[:, 0, NT * REC:NT * REC + NT]
        row_f, col_f, id_f = [b2_rows[:, 0, 256 + n * NT:256 + (n + 1) * NT] for n in range(3)]
        row_no, col_no, slot_no = (b2_rows[:, 1, 0:P], b2_rows[:, 1, P:P + COLS], b2_rows[:, 1, 448:448 + COLS])
        id_i, row_i32, col_i32, slot_i32 = [desk[:, 2304 + n * P:2304 + n * P + w].bitcast(I32)
                                            for n, w in enumerate((NT, P, COLS, COLS))]
        slot_id = b2_rows[:, 2, 256:256 + COLS]
        at_row = xn[:, 0].rearrange("p (a r) -> p a r", a=SORT)
        at_col = h[:].rearrange("p k s -> p (k s)")[:, 0:SORT * COLS * REC].rearrange("p (a c r) -> p a c r", a=SORT, r=REC)
        bg_rows = b2_rows[:, 1, 256:256 + E]
        prefer = b2_rows[:, 1, 288:288 + E]
        tile_no = b2_rows[:, 1, 320:320 + TILES + 1]
        b1_rows = b2_rows[0:E * KT, 2, 0:P]

        def table(flat, n):
            return flat[:, n * NT * E:(n + 1) * NT * E].rearrange("p (t e) -> p t e", e=E)
        logits, less, expd, hot = [table(h[:].rearrange("p k s -> p (k s)"), n) for n in range(4)]
        cand, *scan = [table(desk, n) for n in range(2, 5)]
        past = desk[:, 1280:1280 + (TILES + 1) * E].rearrange("p (t e) -> p t e", e=E)
        top, first, total = [desk[:, 1536 + n * NT:1536 + (n + 1) * NT] for n in range(3)]
        place_i, col_i, row_i = [desk[:, 1792 + n * NT:1792 + (n + 1) * NT].bitcast(I32) for n in range(3)]
        count, tiles_of, ends, ends2, start = [desk[:, 2048 + n * E:2048 + (n + 1) * E] for n in range(5)]
        count_i, tiles_i = [desk[:, 2112 + n * E:2112 + (n + 1) * E].bitcast(I32) for n in range(2)]
        te_f = desk[:, 2176:2176 + TILES + 1]

        pT = ps("pT", [P, 2, D])
        hidden = ps("hidden", [P, KT, 2 * TOK])
        ph = hidden[:, :, 0:TOK]
        py = ps("py", [P, R, D])
        sorted_ = py[:, 0, 0:COLS * REC].rearrange("p (c r) -> p c r", r=REC)
        lg = [hidden[:, half, 0:NB * E].rearrange("p (t e) -> p t e", e=E) for half in range(2)]
        rank, totals = [hidden[:, 2 + n, 0:NT * E].rearrange("p (t e) -> p t e", e=E) for n in range(2)]

        const_step, const_loaded, wg_loaded = sem("const_step"), sem("const_loaded"), sem("wg_loaded")
        weights_loaded = sem("weights_loaded")
        gx_loaded = [sem("gx_loaded_0"), sem("gx_loaded_1")]
        g_bn, g_stats, g_step, g_ln = sem("g_bn"), sem("g_stats"), sem("g_step"), sem("g_ln")
        g_norm, g_full, g_copied = sem("g_norm"), sem("g_full"), sem("g_copied")
        g_logits, g_taken, b1_full, b1_ready = sem("g_logits"), sem("g_taken"), sem("b1_full"), sem("b1_ready")
        route, less_ready, exp_ready, hot_ready, ranked = (sem("route"), sem("less_ready"), sem("exp_ready"),
                                                           sem("hot_ready"), sem("ranked"))
        experts_ready, numbers_ready = sem("experts_ready"), sem("numbers_ready")
        sort_ready, sort_used, rec_ready = sem("sort_ready"), sem("sort_used"), sem("rec_ready")
        rows_set, cur_ready = sem("rows_set"), sem("cur_ready")
        gathered, scattered, b2_loaded = sems("gathered"), sems("scattered"), sems("b2_loaded")
        w1_high, w1_low, w2_high, w2_low = sem("w1_high"), sem("w1_low"), sem("w2_high"), sem("w2_low")
        normed, t_full, xT_high, xT_low = sem("normed"), sem("t_full"), sem("xT_high"), sem("xT_low")
        h_full, gelu_done, h_high, h_low = sem("h_full"), sem("gelu_done"), sem("h_high"), sem("h_low")
        y_full, y_taken, resid_ready = sem("y_full"), sem("y_taken"), sem("resid_ready")
        waited = sem("waited")

        x_batches = x_in.rearrange("b (t p) d -> b p t d", p=P)
        x_tokens = x_in.rearrange("b s d -> (b s) d")
        out_tokens = x_out.rearrange("b s d -> (b s) d")
        N_CONST = 6
        block = ctx.enter_context(nc.Block())

        @block.sync
        def _(sp):
            for half in range(2):
                sp.dma_start(gx[half], x_batches[half]).then_inc(gx_loaded[half], 16)
            with nc.allow_non_contiguous_dma("the gate's weights, rows of 32 bytes, once"):
                sp.dma_start(wg, Wg.rearrange("(k p) e -> p k e", p=P)).then_inc(wg_loaded, 16)
            sp.dma_start(bg_rows, bg.partition_broadcast(P)).then_inc(const_loaded, 16)
            sp.dma_start(b1_rows, b1.rearrange("e (k p) -> (e k) p", p=P)).then_inc(const_loaded, 16)

            def load_weights(m, e):
                sp.dma_start(W_all[m][:, e], (W1, W2)[m][e].rearrange("(k p) d -> p k d", p=P)).then_inc(weights_loaded, 16)

            load_weights(0, 0)
            load_weights(1, 0)
            with sp.Fori(0, B // 2 - 1) as pair:
                for half in range(2):
                    sp.wait_ge(g_full, 2 * NB * pair + NB * (half + 1))
                    sp.sem_inc(waited, 1)
                    sp.dma_start(gx[half], x_batches[2 * pair + (2 + half)]).then_inc(gx_loaded[half], 16)
                    e = 2 * pair + (1 + half)
                    sp.dma_start(W_all[0][:, bass.ds(e, 1)].rearrange("p o k d -> p (o k) d"),
                                 W1[bass.ds(e, 1)].rearrange("o (k p) d -> p (o k) d", p=P)).then_inc(weights_loaded, 16)
            load_weights(0, E - 1)
            for e in range(1, E - 3):
                load_weights(1, e)
            sp.wait_ge(g_logits, N // P + 2)
            for e in range(E - 3, E):
                load_weights(1, e)
            sp.wait_ge(rec_ready, 1)
            sp.wait_ge(experts_ready, 1)
            def tile(lap, i):
                sp.wait_ge(resid_ready, R * RING * lap + R * (i + 1))
                sp.sem_inc(waited, 1)
                e = sp.value_load(tile_expert[0:1, bass.ds(RING * lap + i, 1)], min_val=0, max_val=E - 1)
                sp.dma_start(b2_rows[:, i], b2[bass.ds(e, 1)].rearrange("o d -> (o d)").partition_broadcast(P)).then_inc(b2_loaded[i], 16)

            with sp.Fori(0, LAPS) as lap:
                for i in range(RING):
                    tile(lap, i)
            for i in range(REST):
                tile(LAPS, i)
            for i in range(RING):
                sp.wait_ge(scattered[i], 16 * R * (LAPS + (i < REST)))
                sp.wait_ge(gathered[i], 16 * R * (LAPS + 1))

        @block.gpsimd
        def _(pool):
            pool.sem_inc(g_copied, 2)
            pool.sem_inc(g_taken, 2)
            pool.sem_inc(resid_ready, R * RING)
            pool.sem_inc(y_full, R)
            pool.sem_inc(y_taken, R)
            pool.memset(ident[:], 0.0).then_inc(const_step, 1)
            pool.memset(earlier, 1.0).then_inc(const_step, 1)
            pool.memset(ones, 1.0).then_inc(const_step, 1)
            for n, value in enumerate((EPS, -0.5, -1.0)):
                op = pool.memset(ln_const[:, n], value)
            op.then_inc(const_step, 1)
            pool.wait_ge(const_step, 4)
            pool.affine_select(out=ident[:], in_=ident[:], compare_op=ALU.not_equal, fill=1.0, base=0,
                               pattern=[[-1, P]], channel_multiplier=1).then_inc(const_step, 1)
            pool.affine_select(out=earlier, in_=earlier, compare_op=ALU.is_ge, fill=0.0, base=-1,
                               pattern=[[1, P]], channel_multiplier=-1).then_inc(const_step, 1)
            pool.iota(id_i, pattern=[[P, NT]], base=-NO_ROW, channel_multiplier=1).then_inc(route, 1)
            pool.iota(row_i32, pattern=[[1, P]], base=0, channel_multiplier=0).then_inc(route, 1)
            pool.iota(col_i32, pattern=[[1, COLS]], base=0, channel_multiplier=0).then_inc(route, 1)
            pool.iota(slot_i32, pattern=[[P, COLS]], base=NO_ROW, channel_multiplier=1).then_inc(route, 1)
            for e in range(E):
                pool.memset(prefer[:, e:e + 1], float(E - e)).then_inc(route, 1)
            for t in range(TILES + 1):
                pool.memset(tile_no[:, t:t + 1], float(t)).then_inc(route, 1)

            def layernorm_scale(b, half):
                pool.wait_ge(g_stats, b + 1)
                pool.tensor_tensor(rstd[:, half], mv[:, half, :, 1], ln_const[:, 0], ALU.add).then_inc(g_step, 1)
                pool.wait_ge(g_step, 3 * b + 1)
                pool.tensor_tensor(rstd[:, half], rstd[:, half], ln_const[:, 1], ALU.pow).then_inc(g_step, 1)
                pool.wait_ge(g_step, 3 * b + 2)
                pool.tensor_tensor(nmr[:, half], mv[:, half, :, 0], rstd[:, half], ALU.mult).then_inc(g_step, 1)
                pool.wait_ge(g_step, 3 * b + 3)
                pool.tensor_tensor(nmr[:, half], nmr[:, half], ln_const[:, 2], ALU.mult).then_inc(g_ln, 1)

            with pool.Fori(0, B // 2) as pair:
                for half in range(2):
                    layernorm_scale(2 * pair + half, half)

            pool.wait_ge(experts_ready, 1)
            pool.memset(rows[:], 0.0).then_inc(rows_set, 1)
            pool.wait_ge(rows_set, 1)
            pool.wait_ge(rec_ready, 1)

            def gather(t, i):
                pool.tensor_copy(cur[:, i], rec_all[:, bass.ds(t * R, R)]).then_inc(cur_ready, 1)
                pool.wait_ge(cur_ready, t + 1)
                pool.sem_inc(waited, 1)
                for r in range(R):
                    pool.indirect_dma_start(rows[:, i, r], None, x_tokens,
                                            bass.IndirectOffsetOnAxis(ap=cur[:, i, r, 0:1].bitcast(I32), axis=0),
                                            bounds_check=N - 1, oob_is_err=False).then_inc(gathered[i], 16)

            for t in range(RING):
                gather(t, t)
            def tile(lap, i, ahead=True):
                t = RING * lap + i
                for r in range(R):
                    pool.wait_ge(y_taken, R * t + (R + r + 1))
                    pool.sem_inc(waited, 1)
                    pool.indirect_dma_start(out_tokens, bass.IndirectOffsetOnAxis(ap=cur[:, i, r, 0:1].bitcast(I32), axis=0),
                                            rows[:, i, r], None, bounds_check=N - 1,
                                            oob_is_err=False).then_inc(scattered[i], 16)
                if ahead:
                    pool.wait_ge(scattered[i], 16 * R * lap + 16 * R)
                    pool.sem_inc(waited, 1)
                    gather(t + RING, i)

            with pool.Fori(0, LAPS) as lap:
                for i in range(RING):
                    tile(lap, i)
            for i in range(REST):
                tile(LAPS, i, ahead=False)

        @block.scalar
        def _(act):
            act.wait_ge(b1_full, 1)
            act.copy(b1_cols[:].rearrange("p e k -> p (e k)"), py[:, 0, 0:E * KT]).then_inc(b1_ready, 1)
            with act.Fori(0, B // 2) as pair:
                for half in range(2):
                    b = 2 * pair + half
                    act.wait_ge(g_ln, b + 1)
                    for t in range(NB):
                        act.activation(gx[half][:, t], gx[half][:, t], ACT.Identity, scale=rstd[:, half, t:t + 1],
                                       bias=nmr[:, half, t:t + 1]).then_inc(g_norm, 1)
                    for t in range(NB):
                        act.wait_ge(g_full, NB * b + (t + 1))
                        act.wait_ge(g_logits, NB * b + (t - 1 + 2))
                        act.copy(gxT[t % 2], pT[:, t % 2]).then_inc(g_copied, 1)
            act.wait_ge(less_ready, 1)
            act.activation(expd, less, ACT.Exp).then_inc(exp_ready, 1)

            def split_high(W, to, e, done, chunks=range(CH)):
                for c in chunks:
                    ks = slice(c * KC, (c + 1) * KC)
                    act.copy(to[0][:, ks], W[:, bass.ds(e, 1), ks].rearrange("p o k d -> p (o k) d")).then_inc(done, 1)

            def expert(t):
                return act.value_load(tile_expert[0:1, bass.ds(t, 1)], min_val=0, max_val=E - 1)

            def normalize(t, i, laps):
                act.wait_ge(gathered[i], 16 * R * laps + 16 * R)
                for r in range(R):
                    act.activation(xn[:, r], rows[:, i, r], ACT.Identity, scale=cur[:, i, r, 2:3],
                                   bias=cur[:, i, r, 3:4]).then_inc(normed, 1)

            def high_of_x(t):
                for r in range(R):
                    act.wait_ge(t_full, R * t + (r + 1))
                    act.copy(xT[0][:, :, r * P:(r + 1) * P], pT[:, r].rearrange("p (k s) -> p k s", k=KT)).then_inc(xT_high, 1)

            act.preload_act_table(ACT.Gelu)
            act.wait_ge(experts_ready, 1)
            act.wait_ge(weights_loaded, 16 * 2 * E)
            split_high(W_all[0], w1, expert(0), w1_high)
            normalize(0, 0, 0)
            high_of_x(0)
            def tile(lap, i, last=False):
                t = RING * lap + i
                act.wait_ge(y_full, R * t + R)
                act.sem_inc(waited, 1)
                e = expert(t)
                split_high(W_all[1], w2, e, w2_high)
                if not last:
                    normalize(t + 1, (i + 1) % RING, lap + (i + 1) // RING)
                for f in range(KT):
                    act.wait_ge(h_full, KT * t + (f + 1))
                    act.sem_inc(waited, 1)
                    act.activation(h[:, f], ph[:, f], ACT.Gelu,
                                   bias=b1_cols[:, bass.ds(e, 1), f]).then_inc(gelu_done, 1)
                    act.wait_ge(gelu_done, KT * t + (f + 1))
                    act.copy(hT[0][:, f], h[:, f]).then_inc(h_high, 1)
                if not last:
                    e = expert(t + 1)
                    split_high(W_all[0], w1, e, w1_high, range(CH // 2))
                    high_of_x(t + 1)
                    split_high(W_all[0], w1, e, w1_high, range(CH // 2, CH))

            with act.Fori(0, LAPS) as lap:
                for i in range(RING):
                    tile(lap, i)
            for i in range(REST):
                tile(LAPS, i, last=i == REST - 1)

        @block.vector
        def _(dve):
            dve.wait_ge(const_loaded, 32)
            dve.wait_ge(route, 4 + E + TILES + 1)
            for of, to in ((id_i, id_f), (row_i32, row_no), (col_i32, col_no), (slot_i32, slot_no)):
                dve.tensor_copy(to, of).then_inc(numbers_ready, 1)

            def row_stats(b, half, loads):
                dve.wait_ge(gx_loaded[half], 16 * loads + 16)
                for t in range(NB):
                    dve.bn_stats(stats[:, half, t], gx[half][:, t]).then_inc(g_bn, 1)
                for t in range(NB):
                    dve.wait_ge(g_bn, NB * b + (t + 1))
                    dve.sem_inc(waited, 1)
                    op = dve.bn_aggr(mv[:, half, t], stats[:, half, t])
                op.then_inc(g_stats, 1)

            def take_gate(b, half):
                dve.wait_ge(g_ln, b + 1)
                dve.sem_inc(waited, 1)
                dve.tensor_copy(rec_tok[:, bass.ds(b * NB, NB), 2], rstd[:, half])
                dve.tensor_copy(rec_tok[:, bass.ds(b * NB, NB), 3], nmr[:, half])
                dve.wait_ge(g_logits, NB * b + (NB + 2))
                dve.sem_inc(waited, 1)
                dve.tensor_tensor(logits[:, bass.ds(b * NB, NB)], lg[half],
                                  bg_rows.unsqueeze(1).broadcast_to([P, NB, E]), ALU.add).then_inc(g_taken, 1)

            row_stats(0, 0, 0)
            with dve.Fori(0, B // 2 - 1) as pair:
                for half in range(2):
                    b = 2 * pair + half
                    row_stats(b + 1, 1 - half, pair + half)
                    take_gate(b, half)
            row_stats(B - 1, 1, B // 2 - 1)
            for half in range(2):
                take_gate(B - 2 + half, half)

            def over_experts(a):
                return a.unsqueeze(2).broadcast_to([P, NT, E])

            def over_tiles(a):
                return a.unsqueeze(1).broadcast_to([P, NT, E])

            R0 = 4 + E + TILES + 1
            dve.wait_ge(g_taken, 2 + B)
            dve.tensor_reduce(top, logits, AX_X, ALU.max).then_inc(route, 1)
            dve.wait_ge(route, R0 + 1)
            dve.tensor_tensor(less, logits, over_experts(top), ALU.subtract).then_inc(less_ready, 1)
            dve.wait_ge(less_ready, 1)
            dve.tensor_scalar(cand, less, 0.0, None, ALU.is_equal).then_inc(route, 1)
            dve.wait_ge(route, R0 + 2)
            dve.tensor_tensor(cand, cand, over_tiles(prefer), ALU.mult).then_inc(route, 1)
            dve.wait_ge(route, R0 + 3)
            dve.tensor_reduce(first, cand, AX_X, ALU.max).then_inc(route, 1)
            dve.wait_ge(route, R0 + 4)
            dve.tensor_tensor(hot, over_tiles(prefer), over_experts(first), ALU.is_equal).then_inc(hot_ready, 1)
            dve.wait_ge(exp_ready, 1)
            dve.tensor_reduce(total, expd, AX_X, ALU.add).then_inc(route, 1)
            dve.wait_ge(route, R0 + 5)
            dve.reciprocal(rec_tok[:, :, 1], total).then_inc(route, 1)
            dve.wait_ge(ranked, 1)
            dve.tensor_copy(scan[0], totals).then_inc(route, 1)
            now, n, reach = 0, R0 + 7, 1
            while reach < NT:
                dve.wait_ge(route, n)
                dve.tensor_copy(scan[1 - now][:, 0:reach], scan[now][:, 0:reach]).then_inc(route, 1)
                dve.tensor_tensor(scan[1 - now][:, reach:NT], scan[now][:, reach:NT], scan[now][:, 0:NT - reach],
                                  ALU.add).then_inc(route, 1)
                now, n, reach = 1 - now, n + 2, 2 * reach
            dve.wait_ge(route, n)
            dve.tensor_scalar(count, scan[now][:, NT - 1], float(TOK - 1), None, ALU.add).then_inc(route, 1)
            dve.wait_ge(route, n + 1)
            dve.tensor_copy(count_i, count).then_inc(route, 1)
            dve.wait_ge(route, n + 2)
            dve.tensor_scalar(tiles_i, count_i, TOK.bit_length() - 1, None, ALU.arith_shift_right).then_inc(route, 1)
            dve.wait_ge(route, n + 3)
            dve.tensor_copy(tiles_of, tiles_i).then_inc(route, 1)
            dve.wait_ge(route, n + 4)
            dve.tensor_copy(ends, tiles_of).then_inc(route, 1)
            n, both, now_e, reach = n + 5, [ends, ends2], 0, 1
            while reach < E:
                dve.wait_ge(route, n)
                dve.tensor_copy(both[1 - now_e][:, 0:reach], both[now_e][:, 0:reach]).then_inc(route, 1)
                dve.tensor_tensor(both[1 - now_e][:, reach:E], both[now_e][:, reach:E], both[now_e][:, 0:E - reach],
                                  ALU.add).then_inc(route, 1)
                now_e, n, reach = 1 - now_e, n + 2, 2 * reach
            dve.wait_ge(route, n)
            end = both[now_e]
            dve.tensor_tensor(start, end, tiles_of, ALU.subtract).then_inc(route, 1)
            dve.wait_ge(route, n + 1)
            dve.tensor_scalar(start, start, float(TOK), None, ALU.mult).then_inc(route, 1)
            dve.tensor_tensor(cand, scan[now], totals, ALU.subtract).then_inc(route, 1)
            dve.wait_ge(route, n + 3)
            dve.tensor_tensor(cand, cand, rank, ALU.add).then_inc(route, 1)
            dve.wait_ge(route, n + 4)
            dve.tensor_tensor(cand, cand, over_tiles(start), ALU.add).then_inc(route, 1)
            dve.wait_ge(route, n + 5)
            dve.tensor_tensor(cand, cand, hot, ALU.mult).then_inc(route, 1)
            dve.wait_ge(route, n + 6)
            dve.tensor_reduce(place_of, cand, AX_X, ALU.add).then_inc(route, 1)
            dve.wait_ge(route, n + 7)
            dve.tensor_copy(place_i, place_of).then_inc(route, 1)
            dve.wait_ge(route, n + 8)
            dve.tensor_scalar(col_i, place_i, P.bit_length() - 1, None, ALU.arith_shift_right).then_inc(route, 1)
            dve.tensor_scalar(row_i, place_i, P - 1, None, ALU.bitwise_and).then_inc(route, 1)
            dve.wait_ge(route, n + 10)
            dve.tensor_copy(col_f, col_i).then_inc(route, 1)
            dve.tensor_copy(row_f, row_i).then_inc(route, 1)
            dve.wait_ge(numbers_ready, 4)
            dve.tensor_tensor(rec_tok[:, :, 0], id_f, place_of, ALU.subtract).then_inc(route, 1)
            dve.tensor_tensor(past, tile_no.unsqueeze(2).broadcast_to([P, TILES + 1, E]),
                              end.unsqueeze(1).broadcast_to([P, TILES + 1, E]), ALU.is_ge).then_inc(route, 1)
            dve.wait_ge(route, n + 14)
            dve.tensor_reduce(te_f, past, AX_X, ALU.add).then_inc(route, 1)
            dve.wait_ge(route, n + 15)
            dve.tensor_scalar(te_f, te_f, float(E - 1), None, ALU.min).then_inc(route, 1)
            dve.wait_ge(route, n + 16)
            dve.tensor_copy(tile_expert[:], te_f).then_inc(experts_ready, 1)
            with dve.Fori(0, NT // SORT) as lap:
                for a in range(SORT):
                    t = SORT * lap + a
                    dve.wait_ge(sort_used, t + 1)
                    dve.sem_inc(waited, 1)
                    dve.tensor_scalar(at_row[:, a], row_no, row_f[:, bass.ds(t, 1)], None, ALU.is_equal).then_inc(sort_ready, 1)
                    dve.scalar_tensor_tensor(out=at_col[:, a], in0=col_no.unsqueeze(2).broadcast_to([P, COLS, REC]),
                                             scalar=col_f[:, bass.ds(t, 1)],
                                             in1=rec_tok[:, bass.ds(t, 1)].broadcast_to([P, COLS, REC]),
                                             op0=ALU.is_equal, op1=ALU.mult).then_inc(sort_ready, 1)
            dve.wait_ge(sort_used, NT + SORT)
            dve.tensor_copy(rec_all[:, :, 1:REC], sorted_[:, :, 1:REC]).then_inc(route, 1)
            dve.tensor_tensor(slot_id, sorted_[:, :, 0], slot_no, ALU.add).then_inc(route, 1)
            dve.wait_ge(route, n + 18)
            dve.tensor_copy(rec_all[:, :, 0].bitcast(I32), slot_id).then_inc(rec_ready, 1)

            def split_low(W, to, e, high, low, t, chunks=range(CH)):
                for c in chunks:
                    dve.wait_ge(high, CH * t + (c + 1))
                    dve.sem_inc(waited, 1)
                    ks = slice(c * KC, (c + 1) * KC)
                    dve.tensor_tensor(to[1][:, ks], W[:, bass.ds(e, 1), ks].rearrange("p o k d -> p (o k) d"),
                                      to[0][:, ks].bitcast(F32), ALU.subtract).then_inc(low, 1)

            def expert(t):
                return dve.value_load(tile_expert[0:1, bass.ds(t, 1)], min_val=0, max_val=E - 1)

            def low_of_x(t):
                for r in range(R):
                    dve.wait_ge(xT_high, R * t + (r + 1))
                    dve.tensor_tensor(xT[1][:, :, r * P:(r + 1) * P], pT[:, r].rearrange("p (k s) -> p k s", k=KT),
                                      xT[0][:, :, r * P:(r + 1) * P].bitcast(F32), ALU.subtract).then_inc(xT_low, 1)

            dve.wait_ge(experts_ready, 1)
            split_low(W_all[0], w1, expert(0), w1_high, w1_low, 0)
            low_of_x(0)
            def tile(lap, i, last=False):
                t = RING * lap + i
                split_low(W_all[1], w2, expert(t), w2_high, w2_low, t)
                for f in range(KT):
                    dve.wait_ge(h_high, KT * t + (f + 1))
                    dve.tensor_tensor(hT[1][:, f], h[:, f], hT[0][:, f].bitcast(F32), ALU.subtract).then_inc(h_low, 1)
                if not last:
                    e = expert(t + 1)
                    split_low(W_all[0], w1, e, w1_high, w1_low, t + 1, range(CH // 2))
                    low_of_x(t + 1)
                    split_low(W_all[0], w1, e, w1_high, w1_low, t + 1, range(CH // 2, CH))
                dve.wait_ge(normed, R * t + R)
                dve.wait_ge(b2_loaded[i], 16 * lap + 16)
                dve.sem_inc(waited, 1)
                for r in range(R):
                    dve.scalar_tensor_tensor(out=rows[:, i, r], in0=b2_rows[:, i], scalar=cur[:, i, r, 1:2],
                                             in1=rows[:, i, r], op0=ALU.mult, op1=ALU.add).then_inc(resid_ready, 1)
                for r in range(R):
                    dve.wait_ge(resid_ready, R * t + (R * RING + r + 1))
                    dve.wait_ge(y_full, R * t + (R + r + 1))
                    dve.scalar_tensor_tensor(out=rows[:, i, r], in0=py[:, r], scalar=cur[:, i, r, 1:2],
                                             in1=rows[:, i, r], op0=ALU.mult, op1=ALU.add).then_inc(y_taken, 1)

            with dve.Fori(0, LAPS) as lap:
                for i in range(RING):
                    tile(lap, i)
            for i in range(REST):
                tile(LAPS, i, last=i == REST - 1)

        @block.tensor
        def _(pe):
            pe.sem_inc(sort_used, SORT)
            pe.sem_inc(g_logits, 2)
            pe.wait_ge(const_step, N_CONST)
            pe.wait_ge(const_loaded, 32)
            pe.wait_ge(wg_loaded, 16)
            pe.transpose(py[:, 0, 0:E * KT], b1_rows, ident[0:E * KT, 0:E * KT]).then_inc(b1_full, 1)

            def gate(b, half, t):
                if t == 0:
                    pe.wait_ge(g_taken, b + 1)
                pe.wait_ge(g_copied, NB * b + (t + 3))
                for k in range(KT):
                    op = pe.matmul(lg[half][:, t], gxT[t % 2][:, k * P:(k + 1) * P], wg[:, k],
                                   start=k == 0, stop=k == KT - 1)
                op.then_inc(g_logits, 1)

            with pe.Fori(0, B // 2) as pair:
                for half in range(2):
                    b = 2 * pair + half
                    for t in range(NB):
                        pe.wait_ge(g_norm, NB * b + (t + 1))
                        pe.wait_ge(g_copied, NB * b + (t + 1))
                        for k in range(KT):
                            op = pe.transpose(pT[:, t % 2, k * P:(k + 1) * P], gx[half][:, t, k * P:(k + 1) * P], ident[:])
                        op.then_inc(g_full, 1)
                        if t >= 1:
                            gate(b, half, t - 1)
                    gate(b, half, NB - 1)
            pe.wait_ge(hot_ready, 1)
            pe.matmul(rank.rearrange("p t e -> p (t e)"), earlier, hot.rearrange("p t e -> p (t e)"), start=True, stop=True)
            pe.matmul(totals.rearrange("p t e -> p (t e)"), ones, hot.rearrange("p t e -> p (t e)"), start=True, stop=True).then_inc(ranked, 1)

            def sort(lap, first=False, last=False):
                for a in range(SORT):
                    pe.wait_ge(sort_ready, 2 * SORT * lap + 2 * (a + 1))
                    pe.matmul(py[:, 0, 0:COLS * REC], at_row[:, a], at_col[:, a].rearrange("p c r -> p (c r)"),
                              start=first and a == 0, stop=last and a == SORT - 1).then_inc(sort_used, 1)

            sort(0, first=True)
            with pe.Fori(1, NT // SORT - 1) as lap:
                sort(lap)
            sort(NT // SORT - 1, last=True)

            def transposes(t):
                for r in range(R):
                    pe.wait_ge(normed, R * t + (r + 1))
                    for k in range(KT):
                        op = pe.transpose(pT[:, r, k * P:(k + 1) * P], xn[:, r, k * P:(k + 1) * P], ident[:])
                    op.then_inc(t_full, 1)

            transposes(0)
            def tile(lap, i, last=False):
                t = RING * lap + i
                pe.wait_ge(xT_low, R * t + R)
                for f in range(KT):
                    for k in range(KT):
                        if f == 0 and k % KC == 0:
                            pe.wait_ge(w1_low, CH * t + (k // KC + 1))
                        for n, (x, y) in enumerate(SPLIT):
                            op = pe.matmul(ph[:, f], w1[x][:, k, f * P:(f + 1) * P], xT[y][:, k],
                                           start=k == 0 and n == 0, stop=k == KT - 1 and n == len(SPLIT) - 1)
                    op.then_inc(h_full, 1)
                if not last:
                    transposes(t + 1)
                pe.wait_ge(y_taken, R * t + R)
                for k in range(KT):
                    if k % KC == 0:
                        pe.wait_ge(w2_low, CH * t + (k // KC + 1))
                    pe.wait_ge(h_low, KT * t + (k + 1))
                    for r in range(R):
                        for n, (x, y) in enumerate(SPLIT):
                            op = pe.matmul(py[:, r], hT[x][:, k, r * P:(r + 1) * P], w2[y][:, k],
                                           start=k == 0 and n == 0, stop=k == KT - 1 and n == len(SPLIT) - 1)
                        if k == KT - 1:
                            op.then_inc(y_full, 1)

            with pe.Fori(0, LAPS) as lap:
                for i in range(RING):
                    tile(lap, i)
            for i in range(REST):
                tile(LAPS, i, last=i == REST - 1)


def decoder_layer(nc, x, ctx_1024, mask, w_qkv, b_qkv, w_dense, b_dense, Wq, bq, Wk, bk, Wv, bv, Wo, bo_x,
                  Wg, bg, W1, b1, W2, b2, out):
    x1 = nc.dram_tensor("x_after_self", (B, S, D), F32).ap()
    x2 = nc.dram_tensor("x_after_cross", (B, S, D), F32).ap()
    scratch_mask = nc.dram_tensor("mask_rows", (B, S), F32).ap()

    def self_weights():
        def part(k):
            return (w_qkv[k * P:(k + 1) * P, :],
                    lambda w: w[:, k, 0:3].rearrange("p s (h d) -> p s h d", d=HD),
                    lambda raw: raw[:, 0:3 * D].rearrange("p (h s d) -> p s h d", s=3, d=HD))
        dense = (w_dense.rearrange("(t p) d -> p t d", p=P), lambda w: w[:, :, 3],
                 lambda raw: raw.rearrange("p (t d) -> p t d", d=D))
        return [part(k) for k in range(KT)] + [dense]

    def self_biases(nc, eng, bias, loaded):
        cols = b_qkv.rearrange("(g j s d) -> j s d g", g=G, j=J, s=3)
        with nc.allow_non_contiguous_dma("a few hundred biases, once"):
            for j in range(J):
                for s in range(3):
                    eng.dma_start(bias[HD * j:HD * (j + 1), s], cols[j, s]).then_inc(loaded, 16)

    def cross_weights():
        def part(s, w_in):
            return (w_in.rearrange("(t p) d -> p t d", p=P), lambda w: w[:, :, s],
                    lambda raw: raw.rearrange("p (t d) -> p t d", d=D))
        return [part(s, w) for s, w in enumerate((Wq, Wk, Wv, Wo))]

    def cross_biases(nc, eng, bias, loaded):
        with nc.allow_non_contiguous_dma("a few hundred biases, once"):
            for s, v in enumerate((bq, bk, bv)):
                eng.dma_start(bias[:, s], v.rearrange("(g p) -> p g", p=P)).then_inc(loaded, 16)

    attention_layer(nc, "self", True, x, x1, None, None, None, self_weights, self_biases, b_dense)
    attention_layer(nc, "cross", False, x1, x2, ctx_1024, mask, scratch_mask, cross_weights, cross_biases, bo_x)
    expert_layer(nc, x2, out, Wg, bg, W1, b1, W2, b2)


_INS = ["x", "ctx_1024", "mask_BxS2_bk0",
        "L0_attn_w_qkv", "L0_attn_b_qkv", "L0_attn_w_dense", "L0_attn_b_dense",
        "L0_xattn_Wq", "L0_xattn_bq", "L0_xattn_Wk", "L0_xattn_bk", "L0_xattn_Wv", "L0_xattn_bv",
        "L0_xattn_Wo", "L0_xattn_bo",
        "L0_ffn_Wg", "L0_ffn_bg", "L0_ffn_W1", "L0_ffn_b1", "L0_ffn_W2", "L0_ffn_b2"]


def kernel(**inputs):
    import numpy as _np
    import concourse.bacc as _bacc
    from concourse import mybir as _mybir
    from concourse.bass_utils import run_bass_kernel_spmd as _run

    nc = _bacc.Bacc("TRN2", target_bir_lowering=False, num_devices=1)
    arrays, args = {}, []
    for name in _INS:
        a = _np.ascontiguousarray(inputs[name])
        if a.dtype == _np.bool_:
            a = a.view(_np.int32)
        arrays[f"in_{name}_dram"] = a
        args.append(nc.dram_tensor(f"in_{name}_dram", a.shape, _mybir.dt.from_np(a.dtype), kind="ExternalInput").ap())
    args.append(nc.dram_tensor("out_0_dram", (B, S, D), _mybir.dt.float32, kind="ExternalOutput").ap())
    decoder_layer(nc, *args)
    r = _run(nc, [arrays], core_ids=[0])
    return r.results[0]["out_0_dram"]
```
